# Optimizing a Trainium2 kernel written in Bass

```python
import numpy as np
import jax
import jax.numpy as jnp

def _softmax(x, axis=-1):
    return jax.nn.softmax(x, axis=axis)

def _gelu(x):
    return jax.nn.gelu(x, approximate=True)

def _silu(x):
    return jax.nn.silu(x)

def _sigmoid(x):
    return jax.nn.sigmoid(x)

def _layernorm(x, axis=-1, eps=1e-05):
    m = jnp.mean(x, axis=axis, keepdims=True)
    v = jnp.var(x, axis=axis, keepdims=True)
    return (x - m) / jnp.sqrt(v + eps)

def _scatter_add(tgt, idx, src, axis=0):
    return tgt.at[idx].add(src)

def _segment_sum(src, seg, n):
    return jax.ops.segment_sum(src, seg, n)
kernel_name = 'mk_seq_preln_d2_jaxref_r8_522aa0'

def setup_inputs(seed: int=0):
    np.random.seed(seed)
    _w = jnp.asarray

    def _L0_attn_setup():
        import jax, jax.numpy as jnp
        import numpy as np
        import math
        B, N, D, H = (1, 512, 128, 16)
        HS = D // H
        NEG_INF = -10000.0
        key = jax.random.key(seed)
        k1, k2, k3, k4, k5 = jax.random.split(key, 5)
        return {'encodings': jax.random.normal(k1, (B, N, D), dtype=jnp.float32), 'attn_W': jax.random.normal(k2, (D, 3 * D), dtype=jnp.float32) * 0.02, 'attn_b': jax.random.normal(k3, (3 * D,), dtype=jnp.float32) * 0.02, 'out_W': jax.random.normal(k4, (D, D), dtype=jnp.float32) * 0.02, 'out_b': jax.random.normal(k5, (D,), dtype=jnp.float32) * 0.02}
    _L0_attn_in = _L0_attn_setup()

    def _L0_ffn_setup():
        import jax, jax.numpy as jnp
        import numpy as np
        B, T, D, H, E = (4, 256, 128, 256, 8)
        TOP_K = int(E * 0.25)
        key = jax.random.key(seed)
        ks = jax.random.split(key, 6)
        x = jax.random.normal(ks[0], (B, T, D), dtype=jnp.float32)
        gate = jax.random.normal(ks[1], (D, E), dtype=jnp.float32)
        W1 = jax.random.normal(ks[2], (E, D, H), dtype=jnp.float32) * D ** (-0.5)
        b1 = jnp.zeros((E, H), dtype=jnp.float32)
        W2 = jax.random.normal(ks[3], (E, H, D), dtype=jnp.float32) * H ** (-0.5)
        b2 = jnp.zeros((E, D), dtype=jnp.float32)
        return {'x': x, 'gate': gate, 'W1': W1, 'b1': b1, 'W2': W2, 'b2': b2}
    _L0_ffn_in = _L0_ffn_setup()

    def _L1_attn_setup():
        import jax, jax.numpy as jnp
        import numpy as np
        B, S, D, H = (2, 256, 128, 16)
        HD = D // H
        key = jax.random.key(seed)
        k0, k1, k2 = jax.random.split(key, 3)
        return {'x': jax.random.normal(k0, (B, S, D), jnp.float32), 'qkv_w': jax.random.normal(k1, (D, 3 * D), jnp.float32) / np.sqrt(D).astype(np.float32), 'qkv_b': jnp.zeros((3 * D,), jnp.float32), 'out_w': jax.random.normal(k2, (D, D), jnp.float32) / np.sqrt(D).astype(np.float32), 'out_b': jnp.zeros((D,), jnp.float32)}
    _L1_attn_in = _L1_attn_setup()

    def _L1_ffn_setup():
        import jax, jax.numpy as jnp
        import numpy as np
        NUM_EXPERTS = 8
        TOP_K = 2
        key = jax.random.key(seed)
        ks = jax.random.split(key, 5)
        B, L, E, H, N = (2, 256, 128, 256, NUM_EXPERTS)
        return {'x': jax.random.normal(ks[0], (B, L, E), dtype=jnp.float32), 'gate_kernel': jax.random.normal(ks[1], (E, N), dtype=jnp.float32) / np.sqrt(E), 'w0_kernel': jax.random.normal(ks[2], (N, E, H), dtype=jnp.float32) / np.sqrt(E), 'w1_kernel': jax.random.normal(ks[3], (N, E, H), dtype=jnp.float32) / np.sqrt(E), 'wo_kernel': jax.random.normal(ks[4], (N, H, E), dtype=jnp.float32) / np.sqrt(H)}
    _L1_ffn_in = _L1_ffn_setup()
    _d = {'L0_attn_encodings': _L0_attn_in['encodings'], 'L0_attn_attn_W': _L0_attn_in['attn_W'], 'L0_attn_attn_b': _L0_attn_in['attn_b'], 'L0_attn_out_W': _L0_attn_in['out_W'], 'L0_attn_out_b': _L0_attn_in['out_b'], 'L0_ffn_gate': _L0_ffn_in['gate'], 'L0_ffn_W1': _L0_ffn_in['W1'], 'L0_ffn_b1': _L0_ffn_in['b1'], 'L0_ffn_W2': _L0_ffn_in['W2'], 'L0_ffn_b2': _L0_ffn_in['b2'], 'L1_attn_qkv_w': _L1_attn_in['qkv_w'], 'L1_attn_qkv_b': _L1_attn_in['qkv_b'], 'L1_attn_out_w': _L1_attn_in['out_w'], 'L1_attn_out_b': _L1_attn_in['out_b'], 'L1_ffn_gate_kernel': _L1_ffn_in['gate_kernel'], 'L1_ffn_w0_kernel': _L1_ffn_in['w0_kernel'], 'L1_ffn_w1_kernel': _L1_ffn_in['w1_kernel'], 'L1_ffn_wo_kernel': _L1_ffn_in['wo_kernel']}
    _x0 = _d['L0_attn_encodings']
    _d['L0_attn_encodings'] = jax.random.normal(jax.random.fold_in(jax.random.key(seed), 1), (32, 256, 128), dtype=_x0.dtype)
    del _x0
    return _d

def reference(L0_attn_encodings, L0_attn_attn_W, L0_attn_attn_b, L0_attn_out_W, L0_attn_out_b, L0_ffn_gate, L0_ffn_W1, L0_ffn_b1, L0_ffn_W2, L0_ffn_b2, L1_attn_qkv_w, L1_attn_qkv_b, L1_attn_out_w, L1_attn_out_b, L1_ffn_gate_kernel, L1_ffn_w0_kernel, L1_ffn_w1_kernel, L1_ffn_wo_kernel):

    def _L0_attn_ref(encodings, attn_W, attn_b, out_W, out_b):
        import jax, jax.numpy as jnp
        import numpy as np
        import math
        B, N, D, H = (1, 512, 128, 16)
        HS = D // H
        NEG_INF = -10000.0
        b, n, d = encodings.shape
        qkv = encodings @ attn_W + attn_b
        qkv = qkv.reshape(b, n, H, 3 * HS).transpose(0, 2, 1, 3)
        q, k, v = jnp.split(qkv, 3, axis=-1)
        scores = jnp.einsum('bhki,bhqi->bhkq', k, q) / math.sqrt(HS)
        mask = jnp.arange(n)[:, None] <= jnp.arange(n)[None, :]
        scores = jnp.where(mask, scores, jnp.float32(NEG_INF))
        prob = jax.nn.softmax(scores, axis=2)
        combined = jnp.einsum('bhkq,bhkl->bhql', prob, v)
        out = combined.transpose(0, 2, 1, 3).reshape(b, n, d)
        return out @ out_W + out_b

    def _L0_ffn_ref(x, gate, W1, b1, W2, b2):
        import jax, jax.numpy as jnp
        import numpy as np
        B, T, D, H, E = (4, 256, 128, 256, 8)
        TOP_K = int(E * 0.25)
        raw_gate = jax.nn.softmax(jnp.einsum('btd,de->bte', x, gate), axis=-1)
        topk_scores, topk_idx = jax.lax.top_k(raw_gate, TOP_K)
        mask = jax.nn.one_hot(topk_idx, E, dtype=raw_gate.dtype).sum(axis=-2)
        gate_topk = mask * raw_gate
        gate_topk = gate_topk / jnp.maximum(gate_topk.sum(axis=-1, keepdims=True), 1e-12)
        h = jax.nn.relu(jnp.einsum('btd,edh->beth', x, W1) + b1[None, :, None, :])
        expert_out = jnp.einsum('beth,ehd->betd', h, W2) + b2[None, :, None, :]
        out = jnp.einsum('bte,betd->btd', gate_topk, expert_out)
        return out

    def _L1_attn_ref(x, qkv_w, qkv_b, out_w, out_b):
        import jax, jax.numpy as jnp
        import numpy as np
        B, S, D, H = (2, 256, 128, 16)
        HD = D // H
        b, s, d = x.shape
        h, hd = (H, d // H)
        scale = 1.0 / np.sqrt(hd).astype(np.float32)
        qkv = (x @ qkv_w + qkv_b).reshape(b, s, 3, h, hd)
        q, k, v = (qkv[:, :, 0], qkv[:, :, 1], qkv[:, :, 2])
        logits = jnp.einsum('bqhd,bkhd->bhqk', q, k)
        causal_mask = jnp.triu(jnp.ones((s, s), bool), 1)
        logits = jnp.where(causal_mask, -jnp.inf, logits) * scale
        att = jax.nn.softmax(logits, axis=-1)
        out = jnp.einsum('bhqk,bkhd->bqhd', att, v).reshape(b, s, d)
        return out @ out_w + out_b

    def _L1_ffn_ref(x, gate_kernel, w0_kernel, w1_kernel, wo_kernel):
        import jax, jax.numpy as jnp
        import numpy as np
        NUM_EXPERTS = 8
        TOP_K = 2
        B, L, E = x.shape
        gate_logits = jnp.einsum('ble,en->bln', x, gate_kernel)
        top_k_weights, top_k_indices = jax.lax.top_k(gate_logits, TOP_K)
        softmax_probs = jax.nn.softmax(top_k_weights.astype(jnp.float32), axis=-1)
        weights = jnp.zeros_like(gate_logits)
        b_idx = jnp.arange(B)[:, None, None]
        l_idx = jnp.arange(L)[:, None]
        weights = weights.at[b_idx, l_idx, top_k_indices].set(softmax_probs)
        layer_w0 = jnp.einsum('ble,neh->blnh', x, w0_kernel)
        layer_w1 = jnp.einsum('ble,neh->blnh', x, w1_kernel)
        layer_mult = jax.nn.silu(layer_w0) * layer_w1
        intermediate = jnp.einsum('blnh,nhe->blne', layer_mult, wo_kernel)
        output = jnp.einsum('blne,bln->ble', intermediate, weights)
        return output
    x = L0_attn_encodings
    x = x + _L0_attn_ref(_layernorm(x, axis=-1), L0_attn_attn_W, L0_attn_attn_b, L0_attn_out_W, L0_attn_out_b)
    x = x + _L0_ffn_ref(_layernorm(x, axis=-1), L0_ffn_gate, L0_ffn_W1, L0_ffn_b1, L0_ffn_W2, L0_ffn_b2)
    x = x + _L1_attn_ref(_layernorm(x, axis=-1), L1_attn_qkv_w, L1_attn_qkv_b, L1_attn_out_w, L1_attn_out_b)
    x = x + _L1_ffn_ref(_layernorm(x, axis=-1), L1_ffn_gate_kernel, L1_ffn_w0_kernel, L1_ffn_w1_kernel, L1_ffn_wo_kernel)
    return x

_drawn_inputs = setup_inputs


def setup_inputs(seed=0):
    import zlib

    import numpy as np

    out = dict(_drawn_inputs(seed))
    spreads = {'L0_ffn_b1': (0.0, 0.1),
     'L0_ffn_b2': (0.0, 0.1),
     'L1_attn_qkv_b': (0.0, 0.1),
     'L1_attn_out_b': (0.0, 0.1)}
    factors = {'L0_attn_attn_b': 2.913}
    for name, (base, spread) in spreads.items():
        noise = np.random.default_rng([zlib.crc32(name.encode()), seed]).standard_normal(out[name].shape)
        drawn = base * np.exp(spread * noise) if base else spread * noise
        out[name] = jnp.asarray(drawn.astype(out[name].dtype))
    for name, factor in factors.items():
        out[name] = (out[name] * factor).astype(out[name].dtype)
    return out
```

```python
from contextlib import ExitStack

import concourse.bass as bass
from concourse import mybir

ALU = mybir.AluOpType
ACT = mybir.ActivationFunctionType
AX = mybir.AxisListType
F32 = mybir.dt.float32
F32R = mybir.dt.float32r
BF16 = mybir.dt.bfloat16

P = 128
D = 128
SEQ = 256
TILES = SEQ // P
HEADS = 16
HD = D // HEADS
GROUPS = 4
SLOTS = HEADS // GROUPS
EXPERTS = 8
HID = 256
CHUNKS = HID // P
EPS = 1e-5
SCALE = float(HD) ** -0.5
FILL = -10000.0
FLOOR = -FILL / SCALE
NEG = -1e30
RING = 3
VG, VC = 137, 32
VW = GROUPS * VG
UNITS = 3 * GROUPS


class Batch:

    def __init__(self, least, loop, count):
        self.exists = least >= 0 and least < count
        self.past = least >= count
        self.least = min(least, count - 1) if loop is None else least
        self.number = self.least if loop is None else loop * RING + least
        self.ring = self.least % RING
        self.turn = self.least // RING if loop is None else loop + least // RING


def pipeline(eng, count, deepest, step):
    first = deepest
    while (count - first) % RING:
        first += 1
    for i in range(first):
        step(lambda back, i=i: Batch(i - back, None, count))
    with eng.Fori(0, (count - first) // RING) as loop:
        for u in range(RING):
            step(lambda back, u=u: Batch(first + u - back, loop, count))
    for i in range(count, count + deepest):
        step(lambda back, i=i: Batch(i - back, None, count))


def build(nc, w, x_dram, out_dram):
    BATCHES = x_dram.shape[0]
    with ExitStack() as ctx:
        def sb(name, shape, dt=F32):
            return ctx.enter_context(nc.sbuf_tensor(name, shape, dt))

        def sem(name):
            return ctx.enter_context(nc.semaphore(name))

        X = sb("X", [P, BATCHES * TILES, D])
        kz = sb("kz", [P, RING, HEADS, SEQ], F32R)
        q_stack = sb("q_stack", [P, RING, GROUPS, SEQ], F32R)
        k_stack = sb("k_stack", [P, RING, GROUPS, SEQ], F32R)
        probs = sb("probs", [P, GROUPS, SLOTS, 3 * P])
        v_pad = sb("v_pad", [P, RING, TILES, VW])
        qk_hi = sb("qk_hi", [P, 2, SEQ], F32R)
        qk_lo = sb("qk_lo", [P, 2, SEQ], F32R)
        xn = sb("xn", [P, TILES, D])
        xt_hi = sb("xt_hi", [P, RING, SEQ], F32R)
        xt_lo = sb("xt_lo", [P, RING, SEQ], F32R)
        stats = sb("stats", [P, TILES, 6])
        mv = sb("mv", [P, TILES, 2])
        var_eps = sb("var_eps", [P, TILES])
        rstd = sb("rstd", [P, TILES])
        minus_half = sb("minus_half", [P, TILES])
        neg_max = sb("neg_max", [P, RING, 3, HEADS])
        neg_m = sb("neg_m", [P, RING, TILES, HEADS])
        m_pad = sb("m_pad", [P, TILES, P], F32R)
        floor1 = sb("floor1", [P, 1])
        fill_bias = sb("fill_bias", [P, 1])
        c_fill = sb("c_fill", [P, RING, TILES, HEADS])
        c_u = sb("c_u", [P, RING, TILES * SLOTS, GROUPS, HD + 1])
        o_rows = sb("o_rows", [P, 2, SEQ])
        o_sum = sb("o_sum", [P, TILES * SLOTS, GROUPS, HD + 1])
        o_rden = sb("o_rden", [P, TILES * SLOTS * GROUPS])
        o_norm = sb("o_norm", [P, TILES, D])
        o_t = sb("o_t", [P, SEQ])
        ident = sb("ident", [P, P])
        ident_b = sb("ident_b", [P, P], BF16)
        mask_b = sb("mask_b", [P, SLOTS, P], BF16)
        later = sb("later", [P, 2, P])
        sel = sb("sel", [P, 4, GROUPS, P], F32R)
        sel_f = probs[:, 0, :, :].rearrange("p a b -> p (a b)")[:, 0:GROUPS * P].rearrange("p (g o) -> p g o", g=GROUPS)
        one_rows = sb("one_rows", [P, HEADS])
        w_raw = sb("w_raw", [P, 2, 3, D])
        w_hi = sb("w_hi", [P, 2, 3, D], F32R)
        w_lo = sb("w_lo", [P, 2, 3, D], F32R)
        w_out = sb("w_out", [P, 2, D])
        b_qk = sb("b_qk", [P, 2, 2])
        b_v = sb("b_v", [P, 2, D])
        b_out = sb("b_out", [P, 2, D])
        gate_raw = sb("gate_raw", [P, 2, EXPERTS])
        gate_hi = sb("gate_hi", [P, 2, EXPERTS], F32R)
        gate_lo = sb("gate_lo", [P, 2, EXPERTS], F32R)
        w_down = sb("w_down", [P, EXPERTS, CHUNKS, D])
        b_up = sb("b_up", [P, EXPERTS, CHUNKS])
        b_down = sb("b_down", [P, D])
        rank = sb("rank", [P, TILES, EXPERTS])
        base_e = sb("base_e", [P, TILES, EXPERTS])
        gt = {k: sb(f"g_{k}", [P, TILES, EXPERTS]) for k in
              ("t", "e", "hot", "key", "sel1", "t2", "hot2", "key2", "sel2", "both", "we")}
        gs = {k: sb(f"gs_{k}", [P, TILES]) for k in ("v1", "mk1", "v2", "mk2", "sum", "rsum")}
        g_pad = sb("g_pad", [P, RING, TILES, P])
        g_rows = sb("g_rows", [P, SEQ])
        raw_up = probs[:, 0:2, :, :].rearrange("p a b c -> p (a b c)")[:, 0:EXPERTS * HID]
        hid = probs[:, 2, :, :].rearrange("p a b -> p (a b)")[:, 0:2 * CHUNKS * SEQ].rearrange("p (a c t) -> p a c t", a=2, c=CHUNKS)
        silu = probs[:, 3, :, :].rearrange("p a b -> p (a b)")[:, 0:2 * CHUNKS * SEQ].rearrange("p (a c t) -> p a c t", a=2, c=CHUNKS)
        kz_flat = kz[:, :, :, :].rearrange("p a b c -> p (a b c)")
        NUP = EXPERTS * HID
        up_w = [kz_flat[:, i * NUP:(i + 1) * NUP] for i in range(4)]

        ps = ctx.enter_context(nc.psum_tensor("ps", [P, 8, 512], F32))
        BS, BT, BO, BA, BB, BR = (0, 1), (2, 3), 4, 5, 6, 7
        U0, U1, BY, BTR, BG = (0, 1), (2, 3), (4, 5), 6, 7

        names = """ln_mv rstd_ok xn_ok t_ps xt_hi_ok xt_lo_ok qk_ps qk_hi_ok qk_lo_ok e_ps ks_ok qs_ok
            v_ps v_ok s_ps s_max m_ok mt_ps m_rep st_ps p_exp p_sel pv_ok o_rows_ok ot_ps o_norm_ok
            t2_ps o_t_ok y_ps x_ok u_ps c_ok cu_ok os_ok b_ok st_ok ag_ok nm_ok mh_ok rd_ok""".split()
        S = {n: sem("a_" + n) for n in names}
        fnames = """ln_mv rstd_ok xn_ok t_ps xt_hi_ok xt_lo_ok lg_ps t_ok e_ok g_ok gt_ps gr_ok y9_ps y9_ok
            up_ps silu_ok hid_ok y_ps x_ok st_ok ag_ok top""".split()
        F = {n: sem("f_" + n) for n in fnames}
        kz_in = [sem(f"kz_in{r}") for r in range(RING)]
        x_first, x_rest = sem("x_first"), sem("x_rest")
        w_attn = [sem("w_attn0"), sem("w_attn1")]
        w_raw_in = [sem("w_raw_in0"), sem("w_raw_in1")]
        w_gate_in, w_ffn_in, w_split = sem("w_gate_in"), sem("w_ffn_in"), sem("w_split")
        up_in, up_split = sem("up_in"), sem("up_split")
        masks_ok, sel_f_ok, sel_ok, consts_dve, kz_ok = sem("masks_ok"), sem("sel_f_ok"), sem("sel_ok"), sem("consts_dve"), sem("kz_ok")
        kz_zero = sem("kz_zero")
        dve_chain, pool_chain = sem("dve_chain"), sem("pool_chain")
        pool_passed, dve_passed = sem("pool_passed"), sem("dve_passed")
        stored = sem("stored")
        block = ctx.enter_context(nc.Block())

        def after(eng, s, b, per, count, base):
            if b.exists:
                eng.wait_ge(s, b.number * per + (base * per + count))
            elif b.past:
                eng.wait_ge(s, b.number * per + (base * per + per))

        def tiles(b):
            return X[:, bass.ds(b.number * TILES, TILES), :]

        def one_tile(b, t):
            return X[:, b.number * TILES + t, :]

        def v_view(r, kt, n):
            return v_pad[:, r, kt, :].rearrange("p (g x) -> p g x", g=GROUPS)[:, :, 0:SLOTS * VC]\
                .rearrange("p g (c y) -> p g c y", c=SLOTS)[:, :, :, 0:n]

        TURNS = [(BATCHES - r + RING - 1) // RING for r in range(RING)]
        TOP = 15
        FIRST = 4
        x_view = x_dram.rearrange("b (t p) d -> p (b t) d", p=P)
        out_view = out_dram.rearrange("b (t p) d -> p (b t) d", p=P)

        @block.sync
        def _(sp):
            sp.dma_start(X[:, 0:FIRST * TILES, :], x_view[:, 0:FIRST * TILES, :]).then_inc(x_first, 16)
            for layer in range(2):
                sp.dma_start(w_raw[:, layer, :, :], w["qkv_w"][layer]).then_inc(w_raw_in[layer], 16)
                sp.dma_start(b_qk[:, layer, :], w["qk_b"][layer]).then_inc(w_attn[layer], 16)
                sp.dma_start(b_v[:, layer, :], w["v_b"][layer].partition_broadcast(P)).then_inc(w_attn[layer], 16)
                sp.dma_start(w_out[:, layer, :], w["out_w"][layer]).then_inc(w_attn[layer], 16)
                sp.dma_start(b_out[:, layer, :], w["out_b"][layer].partition_broadcast(P)).then_inc(w_attn[layer], 16)
                if layer == 0:
                    sp.dma_start(X[:, FIRST * TILES:, :], x_view[:, FIRST * TILES:, :]).then_inc(x_rest, 16)
            for layer in range(2):
                sp.dma_start(gate_raw[:, layer, :], w["gate"][layer]).then_inc(w_gate_in, 16)
            sp.dma_start(b_up[:, :, :], w["b1"]).then_inc(w_gate_in, 16)
            sp.wait_ge(consts_dve, 1)
            sp.dma_start(b_down[0:EXPERTS, :], w["b2"]).then_inc(w_gate_in, 16)

            for layer in range(2):
                base = layer * BATCHES

                def step(at):
                    b = at(0)
                    if b.exists:
                        after(sp, S["ks_ok"], b, 2, 2, base)
                        after(sp, S["st_ps"], at(RING), UNITS, UNITS, base)
                        if b.least == 0:
                            sp.wait_ge(kz_zero, layer + 1)
                        for part in range(3):
                            for c in range(SLOTS):
                                row = 32 * part + HD * c
                                dst = kz[row:row + HD, b.ring, :, :].rearrange("p (g c) t -> p g c t", c=SLOTS)[:, :, c, :]
                                sp.dma_start(dst.bitcast(F32), k_stack[row:row + HD, b.ring, :, :].bitcast(F32))\
                                  .then_inc(kz_in[b.ring], 16)
                pipeline(sp, BATCHES, 4, step)

                sp.wait_ge(S["x_ok"], BATCHES * (layer + 1))
                sp.dma_start(w_down[:, :, :, :], w["down"][layer].rearrange("e (c p) d -> p e c d", p=P)).then_inc(w_ffn_in, 16)
                for i, up in enumerate(w["up"][layer]):
                    if i:
                        sp.wait_ge(up_split, 4)
                    sp.dma_start(raw_up.rearrange("p (e h) -> p e h", e=EXPERTS), up.rearrange("e d h -> d e h")).then_inc(up_in, 16)
                if layer == 0:
                    sp.wait_ge(F["x_ok"], BATCHES * EXPERTS)
            for b in range(0, BATCHES, 4):
                sp.wait_ge(F["x_ok"], EXPERTS * (BATCHES + b + 4))
                sp.dma_start(out_view[:, b * TILES:(b + 4) * TILES, :], X[:, b * TILES:(b + 4) * TILES, :]).then_inc(stored, 16)
            sp.wait_ge(stored, 16 * (BATCHES // 4))

        @block.gpsimd
        def _(pool):
            done = [0]

            def link(ins):
                done[0] += 1
                ins.then_inc(pool_chain, 1)
                pool.wait_ge(pool_chain, done[0])

            nc.gpsimd.memset(minus_half[:, :], -0.5)
            link(nc.gpsimd.memset(ident[:, :], 0.0))
            link(nc.gpsimd.affine_select(out=ident[:, :], in_=ident[:, :], compare_op=ALU.not_equal, fill=1.0,
                                         base=0, pattern=[[-1, P]], channel_multiplier=1))
            nc.gpsimd.tensor_copy(ident_b[:, :], ident[:, :]).then_inc(masks_ok, 1)
            for kind, parts in enumerate(((0, 1), (2,), (0, 2), (1,))):
                if kind:
                    pool.wait_ge(sel_ok, kind)
                link(nc.gpsimd.memset(sel_f, 0.0))
                for part in parts:
                    for g in range(GROUPS):
                        view = sel_f[:, g, 32 * part:32 * part + 32]
                        ins = nc.gpsimd.affine_select(out=view, in_=view, compare_op=ALU.not_equal, fill=1.0,
                                                      base=-32 * g, pattern=[[-1, 32]], channel_multiplier=1)
                ins.then_inc(sel_f_ok, 1)
            link(nc.gpsimd.memset(mask_b[:, :, :], 0.0))
            nc.gpsimd.affine_select(out=mask_b[:, :, :], in_=mask_b[:, :, :], compare_op=ALU.is_ge, fill=NEG,
                                    base=0, pattern=[[0, SLOTS], [-1, P]], channel_multiplier=1).then_inc(masks_ok, 1)
            link(nc.gpsimd.memset(later[:, :, :], 1.0))
            nc.gpsimd.affine_select(out=later[:, 0, :], in_=later[:, 0, :], compare_op=ALU.is_gt, fill=0.0,
                                    base=0, pattern=[[-1, P]], channel_multiplier=1).then_inc(masks_ok, 1)
            link(nc.gpsimd.memset(floor1[:, :], FLOOR))
            nc.gpsimd.affine_select(out=floor1[:, :], in_=floor1[:, :], compare_op=ALU.not_equal, fill=3e38,
                                    base=-(P - 1), pattern=[[0, 1]], channel_multiplier=1).then_inc(masks_ok, 1)
            link(nc.gpsimd.memset(one_rows[:, :], 1.0))
            link(nc.gpsimd.affine_select(out=one_rows[:, :], in_=one_rows[:, :], compare_op=ALU.is_ge, fill=0.0,
                                         base=-96, pattern=[[-2, HEADS]], channel_multiplier=1))
            nc.gpsimd.affine_select(out=one_rows[:, :], in_=one_rows[:, :], compare_op=ALU.is_ge, fill=0.0,
                                    base=97, pattern=[[2, HEADS]], channel_multiplier=-1).then_inc(masks_ok, 1)
            for layer in range(2):
                base = layer * BATCHES
                if layer:
                    pool.wait_ge(F["x_ok"], BATCHES * EXPERTS)
                for r in range(RING):
                    ins = nc.gpsimd.memset(kz[:, r, :, :].bitcast(F32), 0.0)
                ins.then_inc(kz_zero, 1)

                def rstd_of(b, M):
                    after(pool, M["ln_mv"], b, 1, 1, base)
                    nc.gpsimd.tensor_tensor(rstd[:, :], var_eps[:, :], minus_half[:, :], ALU.pow).then_inc(M["rstd_ok"], 1)

                def select_unit(b, g, kind):
                    after(pool, S["p_exp"], b, UNITS, 3 * g + kind + 1, base)
                    pool.sem_inc(pool_passed)
                    view = probs[:, g, :, (kind - 1) * SEQ:(kind - 1) * SEQ + P]
                    nc.gpsimd.affine_select(out=view, in_=view, compare_op=ALU.is_ge, fill=0.0, base=0,
                                            pattern=[[0, SLOTS], [1, P]], channel_multiplier=-1).then_inc(S["p_sel"], 1)

                def step(at):
                    b0, b2, b3 = at(0), at(2), at(3)
                    if b0.exists:
                        rstd_of(b0, S)
                    for slot in range(12):
                        if slot == 2 and b0.exists:
                            after(pool, S["xn_ok"], b0, 1, 1, base)
                            nc.gpsimd.tensor_tensor(tiles(b0), tiles(b0), b_out[:, layer, :].unsqueeze(1).broadcast_to([P, TILES, D]),
                                                    ALU.add).then_inc(S["b_ok"], 1)
                        b, u = (b2, slot - 9) if slot >= 9 else (b3, slot + 3)
                        if b.exists and u % 3:
                            select_unit(b, u // 3, u % 3)
                pipeline(pool, BATCHES, 4, step)

                def fstep(at):
                    b0 = at(0)
                    if b0.exists:
                        rstd_of(b0, F)
                        after(pool, F["t_ok"], b0, 1, 1, base)
                        nc.gpsimd.tensor_tensor(gt["e"][:, :, :], base_e[:, :, :], gt["t"][:, :, :], ALU.pow).then_inc(F["e_ok"], 1)
                pipeline(pool, BATCHES, 2, fstep)

        @block.scalar
        def _(act):
            def norm_t_hi(b, M, base):
                after(act, M["t_ps"], b, 1, 1, base)
                nc.scalar.activation(xt_hi[:, b.ring, :], ps[:, BB if M is S else BTR, 0:SEQ], ACT.Copy).then_inc(M["xt_hi_ok"], 1)

            for layer in range(2):
                base = layer * BATCHES
                act.wait_ge(masks_ok, 5)
                act.wait_ge(w_attn[layer], 64)
                act.wait_ge(consts_dve, 1)
                act.wait_ge(kz_zero, layer + 1)
                for r in range(RING):
                    ins = nc.scalar.activation(kz[96:P, r, :, :], one_rows[96:P, :].unsqueeze(2).broadcast_to([32, HEADS, SEQ]), ACT.Copy)
                ins.then_inc(kz_ok, 1)

                def step(at):
                    b0, b2, b3, b4 = at(0), at(2), at(3), at(4)
                    for slot in range(12):
                        if slot == 0 and b4.exists:
                            after(act, S["pv_ok"], b4, GROUPS, GROUPS, base)
                            after(act, S["ot_ps"], at(5), 1, 1, base)
                            nc.scalar.activation(o_rows[:, :, :].rearrange("p a t -> p (a t)"), ps[:, BO, :], ACT.Copy)\
                              .then_inc(S["o_rows_ok"], 1)
                        if slot == 2 and b4.exists and layer == 1:
                            after(act, S["ot_ps"], b4, 1, 1, base)
                            nc.scalar.activation(o_sum[:, :, 0:3, :], ps[:, BR, 0:SEQ].rearrange("p (a b) -> p a b", b=32)[:, :, 0:27].rearrange("p a (g r) -> p a g r", g=3), ACT.Copy)
                            nc.scalar.activation(o_sum[:, :, 3, :], ps[:, BR, SEQ:2 * SEQ].rearrange("p (a b) -> p a b", b=32)[:, :, 0:HD + 1], ACT.Copy)\
                              .then_inc(S["os_ok"], 1)
                        if slot == 4 and b4.exists:
                            after(act, S["t2_ps"], b4, 1, 1, base)
                            nc.scalar.activation(o_t[:, :], ps[:, BR, 0:SEQ], ACT.Copy).then_inc(S["o_t_ok"], 1)
                        if slot == 2 and b0.exists:
                            norm_t_hi(b0, S, base)
                        if slot == 4 and b0.exists:
                            after(act, S["qk_ps"], b0, 1, 1, base)
                            for t in range(2):
                                ins = nc.scalar.activation(qk_hi[:, t, :], ps[:, BA, t * SEQ:(t + 1) * SEQ], ACT.Identity, bias=b_qk[:, layer, t:t + 1])
                            ins.then_inc(S["qk_hi_ok"], 1)
                        if slot in (6, 8, 9, 10) and b0.exists:
                            e = (6, 8, 9, 10).index(slot)
                            after(act, S["e_ps"], b0, 4, e + 1, base)
                            dst = (k_stack if e < 2 else q_stack)[:, b0.ring, 2 * (e % 2):2 * (e % 2) + 2, :]
                            if e == 0:
                                p = at(RING)
                                if p.exists:
                                    act.wait_ge(kz_in[p.ring], (p.turn + (layer * TURNS[p.ring] + 1)) * 192)
                            if e == 2:
                                after(act, S["st_ps"], at(RING), UNITS, UNITS, base)
                            nc.scalar.activation(dst, ps[:, BA if e % 2 == 0 else BB, :].rearrange("p (g t) -> p g t", g=2), ACT.Copy)\
                              .then_inc(S["ks_ok" if e < 2 else "qs_ok"], 1)
                        if slot == 7 and b2.exists:
                            after(act, S["mt_ps"], b2, 1, 1, base)
                            after(act, S["s_ps"], b2, UNITS, UNITS, base)
                            nc.scalar.activation(q_stack[96:P, b2.ring, :, :], ps[96:P, BB, 0:SEQ].unsqueeze(1).broadcast_to([32, GROUPS, SEQ]), ACT.Copy)\
                              .then_inc(S["m_rep"], 1)
                            if layer == 0:
                                after(act, S["cu_ok"], at(2 + RING), 1, 1, base)
                                nc.scalar.activation(c_fill[:, b2.ring, :, :], neg_m[:, b2.ring, :, :], ACT.Exp, bias=fill_bias[:, :], scale=SCALE)\
                                  .then_inc(S["c_ok"], 1)
                        b, u = (b2, slot - 9) if slot >= 9 else (b3, slot + 3)
                        if b.exists:
                            g, kind = u // 3, u % 3
                            after(act, S["st_ps"], b, UNITS, u + 1, base)
                            p = at(3) if slot >= 9 else at(4)
                            if kind == 0:
                                after(act, S["pv_ok"], p, GROUPS, g + 1, base)
                            dst = (probs[:, g, 0:2, 0:SEQ], probs[:, g, 2:4, 0:SEQ], probs[:, g, :, SEQ:3 * P])[kind]
                            nc.scalar.activation(dst, ps[:, BT[u % 2], :].rearrange("p (c q) -> p c q", q=SEQ if kind < 2 else P), ACT.Exp, scale=SCALE)\
                              .then_inc(S["p_exp"], 1)
                pipeline(act, BATCHES, 4, step)

                def fstep(at):
                    b0, b1 = at(0), at(1)
                    for slot in range(8):
                        if slot == 2 and b0.exists:
                            norm_t_hi(b0, F, base)
                        if slot == 7 and b0.exists and layer == 0:
                            after(act, F["gt_ps"], b0, 1, 1, base)
                            nc.scalar.activation(g_rows[:, :], ps[:, BG, 0:SEQ], ACT.Copy).then_inc(F["gr_ok"], 1)
                        if b1.exists:
                            e = slot
                            after(act, F["up_ps"], b1, EXPERTS, e + 1, base)
                            if layer == 0:
                                if e >= 2:
                                    after(act, F["y_ps"], b1, EXPERTS, e - 1, base)
                                else:
                                    after(act, F["y_ps"], at(2), EXPERTS, EXPERTS - 1 + e, base)
                                for ch in range(CHUNKS):
                                    ins = nc.scalar.activation(hid[:, e % 2, ch, :], ps[:, U0[e % 2], ch * SEQ:(ch + 1) * SEQ], ACT.Relu, bias=b_up[:, e, ch:ch + 1])
                                ins.then_inc(F["hid_ok"], 1)
                            else:
                                if e >= 2:
                                    after(act, F["hid_ok"], b1, EXPERTS, e - 1, base)
                                else:
                                    after(act, F["hid_ok"], at(2), EXPERTS, EXPERTS - 1 + e, base)
                                nc.scalar.activation(silu[:, e % 2, :, :].rearrange("p c t -> p (c t)"), ps[:, U0[e % 2], :], ACT.Silu).then_inc(F["silu_ok"], 1)
                act.wait_ge(w_gate_in, 64)
                act.wait_ge(up_split, 2 if layer == 0 else 6)
                pipeline(act, BATCHES, 2, fstep)

        @block.tensor
        def _(pe):
            pe.wait_ge(masks_ok, 5)
            pe.wait_ge(sel_ok, 4)
            for layer in range(2):
                base = layer * BATCHES
                pe.wait_ge(w_attn[layer], 64)
                pe.wait_ge(consts_dve, 1)

                def turn_norm(b, M, bank):
                    after(pe, M["xn_ok"], b, 1, 1, base)
                    for t in range(TILES):
                        ins = nc.tensor.transpose(ps[:, bank, t * P:(t + 1) * P], xn[:, t, :], ident[:, :])
                    ins.then_inc(M["t_ps"], 1)

                def step(at):
                    b0, b1, b2, b3, b4 = (at(i) for i in range(5))
                    for slot in range(12):
                        b, u = (b1, slot - 6) if slot >= 6 else (b2, slot + 6)
                        if b.exists:
                            g, kind = u // 3, u % 3
                            qt, kt = (0, 1, 1)[kind], (0, 0, 1)[kind]
                            if u == 0:
                                if b.least == 0:
                                    pe.wait_ge(kz_ok, layer + 1)
                                pe.wait_ge(kz_in[b.ring], (b.turn + (layer * TURNS[b.ring] + 1)) * 192)
                                after(pe, S["qs_ok"], b, 2, 2, base)
                            if u >= 2:
                                after(pe, S["s_max"], b, UNITS, u - 1, base)
                            else:
                                after(pe, S["s_max"], at(2), UNITS, UNITS - 1 + u, base)
                            bank = ps[:, BS[u % 2], :]
                            if kind != 1:
                                nc.tensor.matmul(bank, ident_b[:, :], mask_b[:, :, :].rearrange("p c k -> p (c k)"), start=True, stop=False, skip_group_check=True)
                            nc.tensor.matmul(bank, q_stack[:, b.ring, g, qt * P:(qt + 1) * P], kz[:, b.ring, g * SLOTS:(g + 1) * SLOTS, kt * P:(kt + 1) * P],
                                             start=(kind == 1), stop=True, skip_group_check=True).then_inc(S["s_ps"], 1)
                        if slot == 7 and b2.exists:
                            after(pe, S["m_ok"], b2, 1, 1, base)
                            after(pe, S["xt_lo_ok"], b0, 1, 1, base)
                            for t in range(TILES):
                                ins = nc.tensor.transpose(ps[:, BB, t * P:(t + 1) * P], m_pad[:, t, :].bitcast(F32), ident[:, :])
                            ins.then_inc(S["mt_ps"], 1)
                        b, u = (b2, slot - 9) if slot >= 9 else (b3, slot + 3)
                        if b.exists:
                            g, kind = u // 3, u % 3
                            if u == 0:
                                after(pe, S["m_rep"], b, 1, 1, base)
                            if u >= 2:
                                after(pe, S["p_exp"], b, UNITS, u - 1, base)
                            else:
                                after(pe, S["p_exp"], at(3), UNITS, UNITS - 1 + u, base)
                            heads, kt = (range(2), range(2, 4), range(4))[kind], kind // 2
                            for j, c in enumerate(heads):
                                n = SEQ - kt * P
                                ins = nc.tensor.matmul(ps[:, BT[u % 2], j * n:(j + 1) * n], kz[:, b.ring, g * SLOTS + c, kt * P:(kt + 1) * P],
                                                       q_stack[:, b.ring, g, kt * P:], start=True, stop=True, skip_group_check=True)
                            ins.then_inc(S["st_ps"], 1)
                        if slot in (2, 5, 8, 11) and b3.exists:
                            g = (slot - 2) // 3
                            after(pe, S["p_sel"], b3, 2 * GROUPS, 2 * g + 2, base)
                            if g == 0:
                                after(pe, S["v_ok"], b3, 1, 1, base)
                                after(pe, S["o_rows_ok"], b4, 1, 1, base)
                            col = 0 if g < 3 else SEQ
                            for kt in range(TILES):
                                for c in range(SLOTS):
                                    lo = g * P + c * VC if g < 3 else 3 * VG + c * VC
                                    ins = nc.tensor.matmul(ps[32 * c:32 * c + 32, BO, col + kt * P:col + SEQ], v_pad[:, b3.ring, kt, lo:lo + 32],
                                                           probs[:, g, c, 0:SEQ] if kt == 0 else probs[:, g, c, SEQ:3 * P],
                                                           start=(kt == 0 and g in (0, 3)), stop=(kt == 1), skip_group_check=True)
                            ins.then_inc(S["pv_ok"], 1)
                        if slot == 1 and b4.exists:
                            after(pe, S["o_rows_ok"], b4, 1, 1, base)
                            after(pe, S["x_ok"], at(5), 1, 1, base)
                            for half in range(2):
                                for t in range(TILES):
                                    ins = nc.tensor.transpose(ps[:, BR, (2 * half + t) * P:(2 * half + t + 1) * P], o_rows[:, half, t * P:(t + 1) * P], ident[:, :])
                            ins.then_inc(S["ot_ps"], 1)
                        if slot == 3 and b4.exists:
                            after(pe, S["o_norm_ok"], b4, 1, 1, base)
                            for t in range(TILES):
                                ins = nc.tensor.transpose(ps[:, BR, t * P:(t + 1) * P], o_norm[:, t, :], ident[:, :])
                            ins.then_inc(S["t2_ps"], 1)
                        if slot == 5 and b4.exists:
                            after(pe, S["o_t_ok"], b4, 1, 1, base)
                            for t in range(TILES):
                                ins = nc.tensor.matmul(ps[:, BR, SEQ + t * P:SEQ + (t + 1) * P], o_t[:, t * P:(t + 1) * P], w_out[:, layer, :], start=True, stop=True, skip_group_check=True)
                            ins.then_inc(S["y_ps"], 1)
                        if slot == 1 and b1.exists:
                            after(pe, S["qs_ok"], b1, 2, 2, base)
                            after(pe, S["xt_lo_ok"], b1, 1, 1, base)
                            for t in range(TILES):
                                for j, (a, ww) in enumerate(((xt_hi, w_hi), (xt_lo, w_hi), (xt_hi, w_lo))):
                                    ins = nc.tensor.matmul(ps[:, BB, t * P:(t + 1) * P], a[:, b1.ring, t * P:(t + 1) * P], ww[:, layer, 2, :], start=(j == 0), stop=(j == 2), skip_group_check=True)
                            ins.then_inc(S["v_ps"], 1)
                        if slot == 2 and b0.exists:
                            after(pe, S["v_ok"], b1, 1, 1, base)
                            turn_norm(b0, S, BB)
                        if slot == 4 and b0.exists:
                            after(pe, S["xt_lo_ok"], b0, 1, 1, base)
                            if b0.least == 0:
                                pe.wait_ge(w_split, 2 + layer)
                            after(pe, S["qs_ok"], b1, 2, 2, base)
                            if layer == 0:
                                after(pe, S["cu_ok"], b3, 1, 1, base)
                            for t in range(2):
                                for j, (a, ww) in enumerate(((xt_hi, w_hi), (xt_lo, w_hi), (xt_hi, w_lo))):
                                    ins = nc.tensor.matmul(ps[:, BA, t * SEQ:(t + 1) * SEQ], ww[:, layer, t, :], a[:, b0.ring, :], start=(j == 0), stop=(j == 2), skip_group_check=True)
                            ins.then_inc(S["qk_ps"], 1)
                        if slot in (6, 8, 9, 10) and b0.exists:
                            e = (6, 8, 9, 10).index(slot)
                            if e == 0:
                                after(pe, S["qk_lo_ok"], b0, 1, 1, base)
                            if e == 1:
                                after(pe, S["m_rep"], b2, 1, 1, base)
                                if not b2.exists:
                                    after(pe, S["xt_lo_ok"], b0, 1, 1, base)
                            if e >= 2:
                                after(pe, S["ks_ok"], b0, 2, e - 1, base)
                            t = 1 if e < 2 else 0
                            for g2 in range(2):
                                g = 2 * (e % 2) + g2
                                for part, src in enumerate((qk_hi, qk_lo)):
                                    ins = nc.tensor.matmul(ps[:, BA if e % 2 == 0 else BB, g2 * SEQ:(g2 + 1) * SEQ], sel[:, 2 * (e >= 2) + part, g, :], src[:, t, :],
                                                           start=(part == 0), stop=(part == 1), skip_group_check=True)
                            ins.then_inc(S["e_ps"], 1)
                        if slot == 11 and b2.exists and layer == 0:
                            after(pe, S["v_ok"], b2, 1, 1, base)
                            after(pe, S["qs_ok"], b0, 2, 1, base)
                            for t, kt, m, first in ((0, 0, 0, True), (0, 1, 1, False), (1, 1, 0, True)):
                                vv = v_view(b2.ring, kt, HD + 1)
                                ins = nc.tensor.matmul(ps[:, BA, t * 144:(t + 1) * 144], later[:, m, :], vv, start=first, stop=(kt == 1), skip_group_check=True)
                            ins.then_inc(S["u_ps"], 1)
                pipeline(pe, BATCHES, 4, step)

                pe.wait_ge(S["x_ok"], BATCHES * (layer + 1))
                pe.wait_ge(up_split, 2 if layer == 0 else 6)
                pe.wait_ge(w_ffn_in, 16 * (layer + 1))
                pe.wait_ge(w_gate_in, 64)
                ups = 1 if layer == 0 else 2

                def fstep(at):
                    b0, b1, b2 = at(0), at(1), at(2)
                    for slot in range(8):
                        if slot == 0 and b1.exists and layer == 0:
                            after(pe, F["gr_ok"], b1, 1, 1, base)
                            for t in range(TILES):
                                ins = nc.tensor.matmul(ps[:, BG, SEQ + t * P:SEQ + (t + 1) * P], g_rows[:, t * P:(t + 1) * P], b_down[:, :], start=True, stop=True, skip_group_check=True)
                            ins.then_inc(F["y9_ps"], 1)
                        if b1.exists:
                            e = slot
                            if e == 0:
                                after(pe, F["xt_lo_ok"], b1, 1, 1, base)
                            free = F["hid_ok"]
                            if e >= 2:
                                after(pe, free, b1, EXPERTS, e - 1, base)
                            else:
                                after(pe, free, at(2), EXPERTS, EXPERTS - 1 + e, base)
                            for k in range(ups):
                                bank = (U0, U1)[k][e % 2]
                                for ch in range(CHUNKS):
                                    for j, (a, ww) in enumerate(((xt_hi, up_w[2 * k]), (xt_lo, up_w[2 * k]), (xt_hi, up_w[2 * k + 1]))):
                                        ins = nc.tensor.matmul(ps[:, bank, ch * SEQ:(ch + 1) * SEQ], ww[:, e * HID + ch * P:e * HID + (ch + 1) * P], a[:, b1.ring, :], start=(j == 0), stop=(j == 2), skip_group_check=True)
                            ins.then_inc(F["up_ps"], 1)
                        b, e = (b1, slot - 1) if slot else (b2, EXPERTS - 1)
                        if b.exists:
                            after(pe, F["hid_ok"], b, EXPERTS, e + 1, base)
                            if e >= 2:
                                after(pe, F["x_ok"], b, EXPERTS, e - 1, base)
                            elif slot:
                                after(pe, F["x_ok"], b2, EXPERTS, EXPERTS - 1 + e, base)
                            for t in range(TILES):
                                for ch in range(CHUNKS):
                                    ins = nc.tensor.matmul(ps[:, BY[e % 2], t * P:(t + 1) * P], hid[:, e % 2, ch, t * P:(t + 1) * P], w_down[:, e, ch, :], start=(ch == 0), stop=(ch == 1), skip_group_check=True)
                            ins.then_inc(F["y_ps"], 1)
                        if slot == 2 and b0.exists:
                            after(pe, F["xt_lo_ok"], b1, 1, 1, base)
                            turn_norm(b0, F, BTR)
                        if slot == 4 and b0.exists:
                            after(pe, F["xt_lo_ok"], b0, 1, 1, base)
                            if layer == 0:
                                after(pe, F["y9_ok"], b1, 1, 1, base)
                            else:
                                after(pe, F["t_ok"], b1, 1, 1, base)
                            for t in range(TILES):
                                for j, (a, ww) in enumerate(((xt_hi, gate_hi), (xt_lo, gate_hi), (xt_hi, gate_lo))):
                                    ins = nc.tensor.matmul(ps[:, BG, t * EXPERTS:(t + 1) * EXPERTS], a[:, b0.ring, t * P:(t + 1) * P], ww[:, layer, :], start=(j == 0), stop=(j == 2), skip_group_check=True)
                            ins.then_inc(F["lg_ps"], 1)
                        if slot == 7 and b0.exists and layer == 0:
                            after(pe, F["g_ok"], b0, 1, 1, base)
                            for t in range(TILES):
                                ins = nc.tensor.transpose(ps[:, BG, t * P:(t + 1) * P], g_pad[:, b0.ring, t, :], ident[:, :])
                            ins.then_inc(F["gt_ps"], 1)
                pipeline(pe, BATCHES, 2, fstep)

        @block.vector
        def _(dve):
            for r in range(RING):
                nc.vector.memset(v_pad[:, r, :, :], 0.0)
                nc.vector.memset(g_pad[:, r, :, :], 0.0)
            nc.vector.memset(m_pad[:, :, :].bitcast(F32), 0.0)
            nc.vector.memset(fill_bias[:, :], FILL)
            nc.vector.memset(base_e[:, :, :], 2.718281828459045)
            for e in range(EXPERTS):
                nc.vector.memset(rank[:, :, e], float(EXPERTS - e))
            nc.vector.memset(b_down[:, :], 0.0).then_inc(dve_chain, 1)
            dve.wait_ge(dve_chain, 1)
            for r in range(RING):
                for g in range(GROUPS):
                    at = g * VG + HD
                    ins = nc.vector.memset(v_pad[:, r, :, at:at + 3 * VC + 1:VC], 1.0)
            ins.then_inc(consts_dve, 1)
            for kind in range(4):
                dve.wait_ge(sel_f_ok, kind + 1)
                nc.vector.tensor_copy(sel[:, kind, :, :], sel_f).then_inc(sel_ok, 1)
            chain = [1]

            def link(ins):
                chain[0] += 1
                ins.then_inc(dve_chain, 1)
                dve.wait_ge(dve_chain, chain[0])

            for layer in range(2):
                dve.wait_ge(w_raw_in[layer], 16)
                link(nc.vector.tensor_copy(w_hi[:, layer, :, :], w_raw[:, layer, :, :]))
                nc.vector.tensor_tensor(w_lo[:, layer, :, :], w_raw[:, layer, :, :], w_hi[:, layer, :, :].bitcast(F32), ALU.subtract).then_inc(w_split, 1)
            dve.wait_ge(w_gate_in, 64)
            link(nc.vector.tensor_copy(gate_hi[:, :, :], gate_raw[:, :, :]))
            nc.vector.tensor_tensor(gate_lo[:, :, :], gate_raw[:, :, :], gate_hi[:, :, :].bitcast(F32), ALU.subtract).then_inc(w_split, 1)
            dve.wait_ge(masks_ok, 5)

            for layer in range(2):
                base = layer * BATCHES

                dve.wait_ge(w_attn[layer], 64)
                if layer:
                    dve.wait_ge(F["x_ok"], BATCHES * EXPERTS)

                def stats_of(b, M):
                    for t in range(TILES):
                        ins = nc.vector.bn_stats(stats[:, t, :], one_tile(b, t))
                    ins.then_inc(M["st_ok"], 1)
                    after(dve, M["st_ok"], b, 1, 1, base)
                    dve.sem_inc(dve_passed)
                    for t in range(TILES):
                        ins = nc.vector.bn_aggr(mv[:, t, :], stats[:, t, :])
                    ins.then_inc(M["ag_ok"], 1)
                    after(dve, M["ag_ok"], b, 1, 1, base)
                    nc.vector.tensor_scalar(var_eps[:, :], mv[:, :, 1], EPS, None, ALU.add).then_inc(M["ln_mv"], 1)

                def norm_of(b, M):
                    after(dve, M["rstd_ok"], b, 1, 1, base)
                    for t in range(TILES):
                        ins = nc.vector.tensor_scalar(xn[:, t, :], one_tile(b, t), mv[:, t, 0:1], rstd[:, t:t + 1], ALU.subtract, ALU.mult)
                    ins.then_inc(M["xn_ok"], 1)

                def norm_t_lo(b, M):
                    after(dve, M["xt_hi_ok"], b, 1, 1, base)
                    nc.vector.tensor_tensor(xt_lo[:, b.ring, :], ps[:, BB if M is S else BTR, 0:SEQ], xt_hi[:, b.ring, :].bitcast(F32), ALU.subtract).then_inc(M["xt_lo_ok"], 1)

                def step(at):
                    b0, b1, b2, b3, b4 = (at(i) for i in range(5))
                    for slot in range(12):
                        if slot == 0 and b0.exists:
                            if layer == 0 and b0.least == 0:
                                dve.wait_ge(x_first, 16)
                            if layer == 0 and b0.least == FIRST:
                                dve.wait_ge(x_rest, 16)
                            stats_of(b0, S)
                        if slot == 0 and b3.exists and layer == 0:
                            after(dve, S["u_ps"], b3, 1, 1, base)
                            after(dve, S["c_ok"], b3, 1, 1, base)
                            for t in range(TILES):
                                out = c_u[:, b3.ring, t * SLOTS:(t + 1) * SLOTS, :, :]
                                ins = nc.vector.tensor_tensor(out, ps[:, BA, t * 144:(t + 1) * 144].rearrange("p (g c r) -> p c g r", g=GROUPS, c=SLOTS),
                                                              c_fill[:, b3.ring, t, :].rearrange("p (g c) -> p c g", g=GROUPS).unsqueeze(3).broadcast_to([P, SLOTS, GROUPS, HD + 1]), ALU.mult)
                            ins.then_inc(S["cu_ok"], 1)
                        if slot == 6 and b2.exists:
                            nm, m = neg_max[:, b2.ring, :, :], neg_m[:, b2.ring, :, :]
                            after(dve, S["s_max"], b2, UNITS, UNITS, base)
                            if layer == 0:
                                after(dve, S["c_ok"], at(2 + RING), 1, 1, base)
                                nc.vector.tensor_scalar(m[:, 0, :], nm[:, 0, :], FLOOR, None, ALU.min)
                                nc.vector.scalar_tensor_tensor(out=m[:, 1, :], in0=nm[:, 1, :], scalar=floor1[:, 0:1], in1=nm[:, 2, :], op0=ALU.min, op1=ALU.min).then_inc(S["nm_ok"], 1)
                            else:
                                nc.vector.tensor_copy(m[:, 0, :], nm[:, 0, :])
                                nc.vector.tensor_tensor(m[:, 1, :], nm[:, 1, :], nm[:, 2, :], ALU.min).then_inc(S["nm_ok"], 1)
                            after(dve, S["nm_ok"], b2, 1, 1, base)
                            after(dve, S["mt_ps"], at(3), 1, 1, base)
                            nc.vector.tensor_copy(m_pad[:, :, 96:P:2], m).then_inc(S["mh_ok"], 1)
                            after(dve, S["mh_ok"], b2, 1, 1, base)
                            nc.vector.tensor_tensor(m_pad[:, :, 97:P:2], m, m_pad[:, :, 96:P:2].bitcast(F32), ALU.subtract).then_inc(S["m_ok"], 1)
                        b, u = (b1, slot - 6) if slot >= 6 else (b2, slot + 6)
                        if b.exists:
                            g, kind = u // 3, u % 3
                            after(dve, S["s_ps"], b, UNITS, u + 1, base)
                            nc.vector.tensor_reduce(neg_max[:, b.ring, kind, g * SLOTS:(g + 1) * SLOTS], ps[:, BS[u % 2], :].rearrange("p (c k) -> p c k", c=SLOTS),
                                                    AX.X, ALU.max, negate=True).then_inc(S["s_max"], 1)
                        if slot == 1 and b0.exists:
                            after(dve, S["t_ps"], b1, 1, 1, base)
                            norm_of(b0, S)
                        if slot == 2 and b1.exists:
                            after(dve, S["v_ps"], b1, 1, 1, base)
                            after(dve, S["pv_ok"], at(1 + RING), GROUPS, GROUPS, base)
                            for t in range(TILES):
                                ins = nc.vector.tensor_tensor(v_view(b1.ring, t, HD), ps[:, BB, t * P:(t + 1) * P].rearrange("p (g c r) -> p g c r", g=GROUPS, c=SLOTS),
                                                              b_v[:, layer, :].rearrange("p (g c r) -> p g c r", g=GROUPS, c=SLOTS), ALU.add)
                            ins.then_inc(S["v_ok"], 1)
                        if slot == 2 and b4.exists:
                            after(dve, S["ot_ps"], b4, 1, 1, base)
                            if layer == 0:
                                for part, gg in ((0, slice(0, 3)), (1, slice(3, 4))):
                                    src = ps[:, BR, part * SEQ:(part + 1) * SEQ].rearrange("p (a b) -> p a b", b=32)[:, :, 0:9 * (3 if part == 0 else 1)]
                                    ins = nc.vector.tensor_tensor(o_sum[:, :, gg, :].rearrange("p a g r -> p a (g r)"), src, c_u[:, b4.ring, :, gg, :].rearrange("p a g r -> p a (g r)"), ALU.add)
                                ins.then_inc(S["os_ok"], 1)
                            after(dve, S["os_ok"], b4, 1, 1, base)
                            nc.vector.reciprocal(o_rden[:, :], o_sum[:, :, :, :].rearrange("p a g r -> p (a g) r")[:, :, HD]).then_inc(S["rd_ok"], 1)
                            after(dve, S["rd_ok"], b4, 1, 1, base)
                            nc.vector.tensor_tensor(o_norm[:, :, :].rearrange("p t (h r) -> p (t h) r", r=HD), o_sum[:, :, :, :].rearrange("p a g r -> p (a g) r")[:, :, 0:HD],
                                                    o_rden[:, :].unsqueeze(2).broadcast_to([P, TILES * HEADS, HD]), ALU.mult).then_inc(S["o_norm_ok"], 1)
                        if slot == 3 and b0.exists:
                            norm_t_lo(b0, S)
                        if slot == 5 and b0.exists:
                            after(dve, S["qk_hi_ok"], b0, 1, 1, base)
                            for t in range(2):
                                ins = nc.vector.scalar_tensor_tensor(out=qk_lo[:, t, :], in0=ps[:, BA, t * SEQ:(t + 1) * SEQ], scalar=b_qk[:, layer, t:t + 1],
                                                                     in1=qk_hi[:, t, :].bitcast(F32), op0=ALU.add, op1=ALU.subtract)
                            ins.then_inc(S["qk_lo_ok"], 1)
                        if slot == 6 and b4.exists:
                            after(dve, S["y_ps"], b4, 1, 1, base)
                            after(dve, S["b_ok"], b4, 1, 1, base)
                            nc.vector.tensor_tensor(tiles(b4), tiles(b4), ps[:, BR, SEQ:2 * SEQ].rearrange("p (t d) -> p t d", t=TILES), ALU.add).then_inc(S["x_ok"], 1)
                pipeline(dve, BATCHES, 4, step)

                dve.wait_ge(S["x_ok"], BATCHES * (layer + 1))
                for k in range(1 + layer):
                    dve.wait_ge(up_in, 16 * (k + 1 + layer))
                    nc.vector.tensor_copy(up_w[2 * k], raw_up).then_inc(up_split, 1)
                    dve.wait_ge(up_split, 2 * (k + layer) + 1)
                    nc.vector.tensor_tensor(up_w[2 * k + 1], raw_up, up_w[2 * k].bitcast(F32), ALU.subtract).then_inc(up_split, 1)

                def fstep(at):
                    b0, b1, b2 = at(0), at(1), at(2)
                    for slot in range(8):
                        if slot == 0 and b1.exists and layer == 0:
                            after(dve, F["y9_ps"], b1, 1, 1, base)
                            nc.vector.tensor_tensor(tiles(b1), tiles(b1), ps[:, BG, SEQ:2 * SEQ].rearrange("p (t d) -> p t d", t=TILES), ALU.add).then_inc(F["y9_ok"], 1)
                            after(dve, F["y9_ok"], b1, 1, 1, base)
                        b, e = (b1, slot - 1) if slot else (b2, EXPERTS - 1)
                        if b.exists:
                            after(dve, F["y_ps"], b, EXPERTS, e + 1, base)
                            if e:
                                after(dve, F["x_ok"], b, EXPERTS, e, base)
                            for t in range(TILES):
                                ins = nc.vector.scalar_tensor_tensor(out=one_tile(b, t), in0=ps[:, BY[e % 2], t * P:(t + 1) * P], scalar=g_pad[:, b.ring, t, e:e + 1],
                                                                     in1=one_tile(b, t), op0=ALU.mult, op1=ALU.add)
                            ins.then_inc(F["x_ok"], 1)
                        if slot == 0 and b0.exists:
                            stats_of(b0, F)
                        if slot == 1 and b0.exists:
                            after(dve, F["t_ps"], b1, 1, 1, base)
                            norm_of(b0, F)
                        if slot == 3 and b0.exists:
                            norm_t_lo(b0, F)
                        if slot == 5 and b0.exists:
                            top_two(b0)
                        if b1.exists and layer == 1:
                            e = slot
                            after(dve, F["silu_ok"], b1, EXPERTS, e + 1, 0)
                            if e >= 2:
                                after(dve, F["y_ps"], b1, EXPERTS, e - 1, base)
                            else:
                                after(dve, F["y_ps"], at(2), EXPERTS, EXPERTS - 1 + e, base)
                            nc.vector.tensor_tensor(hid[:, e % 2, :, :].rearrange("p c t -> p (c t)"), silu[:, e % 2, :, :].rearrange("p c t -> p (c t)"), ps[:, U1[e % 2], :], ALU.mult).then_inc(F["hid_ok"], 1)

                def top_two(b):
                    count = [0]

                    def chained(ins):
                        count[0] += 1
                        ins.then_inc(F["top"], 1)
                        after(dve, F["top"], b, TOP, count[0], base)

                    def wide(s):
                        return s[:, :].unsqueeze(2).broadcast_to([P, TILES, EXPERTS])
                    logits = ps[:, BG, 0:TILES * EXPERTS].rearrange("p (t e) -> p t e", t=TILES)
                    after(dve, F["lg_ps"], b, 1, 1, base)
                    chained(nc.vector.tensor_reduce(gs["v1"][:, :], logits, AX.X, ALU.max))
                    nc.vector.tensor_tensor(gt["t"][:, :, :], logits, wide(gs["v1"]), ALU.subtract).then_inc(F["t_ok"], 1)
                    after(dve, F["t_ok"], b, 1, 1, base)
                    hots = (("t", "hot", "key", "mk1", "sel1"), ("t2", "hot2", "key2", "mk2", "sel2"))
                    for n, (t, hot, key, mk, se) in enumerate(hots):
                        if n:
                            chained(nc.vector.scalar_tensor_tensor(out=gt["t2"][:, :, :], in0=gt["sel1"][:, :, :], scalar=-3e38, in1=gt["t"][:, :, :], op0=ALU.mult, op1=ALU.add))
                            chained(nc.vector.tensor_reduce(gs["v2"][:, :], gt["t2"][:, :, :], AX.X, ALU.max))
                            chained(nc.vector.tensor_tensor(gt[hot][:, :, :], gt[t][:, :, :], wide(gs["v2"]), ALU.is_ge))
                        else:
                            chained(nc.vector.tensor_scalar(gt[hot][:, :, :], gt[t][:, :, :], 0.0, None, ALU.is_ge))
                        chained(nc.vector.tensor_tensor(gt[key][:, :, :], gt[hot][:, :, :], rank[:, :, :], ALU.mult))
                        chained(nc.vector.tensor_reduce(gs[mk][:, :], gt[key][:, :, :], AX.X, ALU.max))
                        chained(nc.vector.tensor_tensor(gt[se][:, :, :], gt[key][:, :, :], wide(gs[mk]), ALU.is_equal))
                    chained(nc.vector.tensor_tensor(gt["both"][:, :, :], gt["sel1"][:, :, :], gt["sel2"][:, :, :], ALU.add))
                    after(dve, F["e_ok"], b, 1, 1, base)
                    chained(nc.vector.tensor_tensor(gt["we"][:, :, :], gt["both"][:, :, :], gt["e"][:, :, :], ALU.mult))
                    chained(nc.vector.tensor_reduce(gs["sum"][:, :], gt["we"][:, :, :], AX.X, ALU.add))
                    chained(nc.vector.reciprocal(gs["rsum"][:, :], gs["sum"][:, :]))
                    assert count[0] == TOP
                    nc.vector.tensor_tensor(g_pad[:, b.ring, :, 0:EXPERTS], gt["we"][:, :, :], wide(gs["rsum"]), ALU.mult).then_inc(F["g_ok"], 1)
                pipeline(dve, BATCHES, 2, fstep)


def kernel(**inputs):
    import numpy as _np
    import concourse.bacc as _bacc
    from concourse.bass_utils import run_bass_kernel_spmd as _run

    nc = _bacc.Bacc("TRN2", target_bir_lowering=False, num_devices=1)
    arrays = {}

    def dram(name, a):
        a = _np.ascontiguousarray(a)
        arrays[name] = a
        return nc.dram_tensor(name, a.shape, mybir.dt.from_np(a.dtype), kind="ExternalInput").ap()

    i = {k: _np.asarray(v) for k, v in inputs.items()}
    w0, w1 = i["L0_attn_attn_W"], i["L1_attn_qkv_w"]
    b0, b1 = i["L0_attn_attn_b"], i["L1_attn_qkv_b"]
    qkv_b = (b0.reshape(SLOTS, GROUPS, 3, HD).transpose(2, 1, 0, 3).reshape(3, D),
             b1.reshape(3, SLOTS, GROUPS, HD).transpose(0, 2, 1, 3).reshape(3, D))
    w = {
        "qkv_w": [dram("qkv_w0", w0.reshape(D, SLOTS, GROUPS, 3, HD).transpose(0, 3, 2, 1, 4).reshape(D, 3, D)),
                  dram("qkv_w1", w1.reshape(D, 3, SLOTS, GROUPS, HD).transpose(0, 1, 3, 2, 4).reshape(D, 3, D))],
        "qk_b": [dram(f"qk_b{k}", b[0:2].T) for k, b in enumerate(qkv_b)],
        "v_b": [dram(f"v_b{k}", b[2]) for k, b in enumerate(qkv_b)],
        "out_w": [dram("out_w0", i["L0_attn_out_W"]), dram("out_w1", i["L1_attn_out_w"])],
        "out_b": [dram("out_b0", i["L0_attn_out_b"]), dram("out_b1", i["L1_attn_out_b"])],
        "gate": [dram("gate0", i["L0_ffn_gate"]), dram("gate1", i["L1_ffn_gate_kernel"])],
        "up": [[dram("up0", i["L0_ffn_W1"])], [dram("up1", i["L1_ffn_w0_kernel"]), dram("up2", i["L1_ffn_w1_kernel"])]],
        "down": [dram("down0", i["L0_ffn_W2"]), dram("down1", i["L1_ffn_wo_kernel"])],
        "b1": dram("b1", i["L0_ffn_b1"].reshape(EXPERTS, CHUNKS, P).transpose(2, 0, 1)),
        "b2": dram("b2", i["L0_ffn_b2"]),
    }
    x = dram("x", i["L0_attn_encodings"])
    out = nc.dram_tensor("out", x.shape, F32, kind="ExternalOutput").ap()
    build(nc, w, x, out)
    r = _run(nc, [arrays], core_ids=[0])
    return r.results[0]["out"]
```

```python
from contextlib import ExitStack

import concourse.bass as bass
from concourse import mybir

ALU = mybir.AluOpType
ACT = mybir.ActivationFunctionType
AX = mybir.AxisListType
F32 = mybir.dt.float32
F32R = mybir.dt.float32r
BF16 = mybir.dt.bfloat16

P = 128
D = 128
SEQ = 256
TILES = SEQ // P
HEADS = 16
HD = D // HEADS
GROUPS = 4
SLOTS = HEADS // GROUPS
EXPERTS = 8
HID = 256
CHUNKS = HID // P
EPS = 1e-5
SCALE = float(HD) ** -0.5
FILL = -10000.0
FLOOR = -FILL / SCALE
NEG = -1e30
RING = 3
VG, VC = 137, 32
VW = GROUPS * VG
HIDS = 4
UNITS = 3 * GROUPS


class Batch:

    def __init__(self, least, loop, count):
        self.exists = least >= 0 and least < count
        self.past = least >= count
        self.least = min(least, count - 1) if loop is None else least
        self.number = self.least if loop is None else loop * RING + least
        self.ring = self.least % RING
        self.turn = self.least // RING if loop is None else loop + least // RING


def pipeline(eng, count, deepest, step):
    first = deepest
    while (count - first) % RING:
        first += 1
    for i in range(first):
        step(lambda back, i=i: Batch(i - back, None, count))
    with eng.Fori(0, (count - first) // RING) as loop:
        for u in range(RING):
            step(lambda back, u=u: Batch(first + u - back, loop, count))
    for i in range(count, count + deepest):
        step(lambda back, i=i: Batch(i - back, None, count))


def build(nc, w, x_dram, out_dram):
    BATCHES = x_dram.shape[0]
    with ExitStack() as ctx:
        def sb(name, shape, dt=F32):
            return ctx.enter_context(nc.sbuf_tensor(name, shape, dt))

        def sem(name):
            return ctx.enter_context(nc.semaphore(name))

        X = sb("X", [P, BATCHES * TILES, D])
        kz = sb("kz", [P, RING, HEADS, SEQ], F32R)
        q_stack = sb("q_stack", [P, RING, GROUPS, SEQ], F32R)
        k_stack = sb("k_stack", [P, RING, GROUPS, SEQ], F32R)
        probs = sb("probs", [P, GROUPS, SLOTS, 3 * P])
        v_pad = sb("v_pad", [P, RING, TILES, VW])
        qk_hi = sb("qk_hi", [P, 2, SEQ], F32R)
        qk_lo = sb("qk_lo", [P, 2, SEQ], F32R)
        xn = sb("xn", [P, TILES, D])
        xt_hi = sb("xt_hi", [P, RING, SEQ], F32R)
        xt_lo = sb("xt_lo", [P, RING, SEQ], F32R)
        stats = sb("stats", [P, TILES, 6])
        mv = sb("mv", [P, TILES, 2])
        rstd = sb("rstd", [P, TILES])
        var_eps = sb("var_eps", [P, TILES])
        minus_half = sb("minus_half", [P, TILES])
        x_shift = sb("x_shift", [P, TILES])
        neg_max = sb("neg_max", [P, RING, 3, HEADS])
        neg_m = sb("neg_m", [P, RING, TILES, HEADS])
        m_pad = sb("m_pad", [P, TILES, P], F32R)
        floor1 = sb("floor1", [P, 1])
        fill_bias = sb("fill_bias", [P, 1])
        c_fill = sb("c_fill", [P, RING, TILES, HEADS])
        c_u = sb("c_u", [P, RING, TILES * SLOTS, GROUPS, HD + 1])
        o_rows = sb("o_rows", [P, 2, SEQ])
        o_sum = sb("o_sum", [P, TILES * SLOTS, GROUPS, HD + 1])
        o_rden = sb("o_rden", [P, TILES * SLOTS * GROUPS])
        o_norm = sb("o_norm", [P, TILES, D])
        o_t = sb("o_t", [P, SEQ])
        ident = sb("ident", [P, P])
        mask = sb("mask", [P, P])
        later = sb("later", [P, 2, P])
        sel = sb("sel", [P, 4, GROUPS, P], F32R)
        sel_f = probs[:, :, :, :].rearrange("p a b c -> p (a b c)")[:, 0:4 * GROUPS * P].rearrange("p (k g o) -> p k g o", k=4, g=GROUPS)
        one_rows = sb("one_rows", [P, HEADS])
        raw_up = sb("raw_up", [P, EXPERTS, HID])
        w_raw = raw_up[:, :, :].rearrange("p e h -> p (e h)")[:, 0:2 * 3 * D].rearrange("p (l j d) -> p l j d", l=2, j=3)
        w_hi = sb("w_hi", [P, 2, 3, D], F32R)
        w_lo = sb("w_lo", [P, 2, 3, D], F32R)
        w_out = sb("w_out", [P, 2, D])
        b_qk = sb("b_qk", [P, 2, 2])
        b_v = sb("b_v", [P, 2])
        b_out = sb("b_out", [P, 2, D])
        gate_raw = sb("gate_raw", [P, 2, EXPERTS])
        gate_hi = sb("gate_hi", [P, 2, EXPERTS], F32R)
        gate_lo = sb("gate_lo", [P, 2, EXPERTS], F32R)
        w_down = sb("w_down", [P, EXPERTS, CHUNKS, D])
        b_up = sb("b_up", [P, EXPERTS, CHUNKS])
        b_down = sb("b_down", [P, D])
        rank = sb("rank", [P, TILES, EXPERTS])
        base_e = sb("base_e", [P, TILES, EXPERTS])
        gt = {k: sb(f"g_{k}", [P, TILES, EXPERTS]) for k in
              ("t", "e", "hot", "key", "sel1", "t2", "hot2", "key2", "sel2", "both", "we")}
        gs = {k: sb(f"gs_{k}", [P, TILES]) for k in ("v1", "mk1", "v2", "mk2", "sum", "rsum")}
        g_pad = sb("g_pad", [P, RING, TILES, P])
        g_rows = o_t
        raw_up2 = sb("raw_up2", [P, EXPERTS // 2, HID])
        q_flat = q_stack[:, :, :, :].rearrange("p a b c -> p (a b c)")
        k_flat = k_stack[:, :, :, :].rearrange("p a b c -> p (a b c)")
        s_flat = sel[:, :, :, :].rearrange("p a b c -> p (a b c)")
        p_flat = probs[:, :, :, :].rearrange("p a b c -> p (a b c)")

        def up_w(k, part, e):
            if k and part:
                flat, at = (q_flat, k_flat)[e // 4], EXPERTS + e % 4
            else:
                flat, at = (s_flat if k else (q_flat, k_flat)[part]), e
            return flat[:, at * HID:(at + 1) * HID]

        def up_raw(k, e):
            return raw_up[:, e, :] if k == 0 else (raw_up2[:, e, :] if e < EXPERTS // 2 else rest2[:, e - EXPERTS // 2, :])
        rest2 = p_flat[:, 0:EXPERTS // 2 * HID].rearrange("p (e h) -> p e h", h=HID)
        hid = p_flat[:, EXPERTS * HID:(EXPERTS + HIDS * CHUNKS) * HID].rearrange("p (a c t) -> p a c t", a=HIDS, c=CHUNKS)
        silu = p_flat[:, (EXPERTS + HIDS * CHUNKS) * HID:(EXPERTS + HIDS * CHUNKS + 2 * CHUNKS) * HID].rearrange("p (a c t) -> p a c t", a=2, c=CHUNKS)

        ps = ctx.enter_context(nc.psum_tensor("ps", [P, 8, 512], F32))
        BS, BT, BO, BA, BB, BR = (0, 1), (2, 3), 4, 5, 6, 7
        U0, U1, BY, BTR, BG = (0, 1), (2, 3), (4, 5), 6, 7

        names = """ln_mv rstd_ok xn_ok t_ps xt_hi_ok xt_lo_ok qk_ps qk_hi_ok qk_lo_ok e_ps ks_ok qs_ok
            v_ps v_ok s_ps s_max m_ok mt_ps m_rep st_ps p_exp p_sel pv_ok o_rows_ok ot_ps o_norm_ok
            t2_ps o_t_ok y_ps x_ok u_ps c_ok cu_ok os_ok b_ok st_ok ag_ok nm_ok mh_ok rd_ok""".split()
        S = {n: sem("a_" + n) for n in names + ["r_ok"]}
        fnames = """ln_mv rstd_ok xn_ok t_ps xt_hi_ok xt_lo_ok lg_ps t_ok e_ok g_ok gt_ps gr_ok y9_ps y9_ok
            up_ps silu_ok hid_ok y_ps x_ok st_ok ag_ok top""".split()
        F = {n: sem("f_" + n) for n in fnames}
        kz_in = [sem(f"kz_in{r}") for r in range(RING)]
        x_first, x_rest = sem("x_first"), sem("x_rest")
        w_attn = [sem("w_attn0"), sem("w_attn1")]
        w_raw_in = [sem("w_raw_in0"), sem("w_raw_in1")]
        w_gate_in, w_ffn_in, w_split = sem("w_gate_in"), sem("w_ffn_in"), sem("w_split")
        up_in, up2_in, rest2_in, up_hi, up_split = sem("up_in"), sem("up2_in"), sem("rest2_in"), sem("up_hi"), sem("up_split")
        masks_ok, sel_f_ok, sel_ok, consts_dve, kz_ok = sem("masks_ok"), sem("sel_f_ok"), sem("sel_ok"), sem("consts_dve"), sem("kz_ok")
        kz_zero, sel_zero = sem("kz_zero"), sem("sel_zero")
        b_v_wide, b_v_ps, b_out_ok = sem("b_v_wide"), sem("b_v_ps"), sem("b_out_ok")
        dve_chain, pool_chain = sem("dve_chain"), sem("pool_chain")
        pool_passed, dve_passed = sem("pool_passed"), sem("dve_passed")
        stored = sem("stored")
        block = ctx.enter_context(nc.Block())

        def after(eng, s, b, per, count, base):
            if b.exists:
                eng.wait_ge(s, b.number * per + (base * per + count))
            elif b.past:
                eng.wait_ge(s, b.number * per + (base * per + per))

        def tiles(b):
            return X[:, bass.ds(b.number * TILES, TILES), :]

        def one_tile(b, t):
            return X[:, b.number * TILES + t, :]

        def v_view(r, kt, n):
            return v_pad[:, r, kt, :].rearrange("p (g x) -> p g x", g=GROUPS)[:, :, 0:SLOTS * VC]\
                .rearrange("p g (c y) -> p g c y", c=SLOTS)[:, :, :, 0:n]

        TURNS = [(BATCHES - r + RING - 1) // RING for r in range(RING)]
        TOP = 15
        FIRST = 4
        x_view = x_dram.rearrange("b (t p) d -> p (b t) d", p=P)
        out_view = out_dram.rearrange("b (t p) d -> p (b t) d", p=P)

        @block.sync
        def _(sp):
            sp.dma_start(X[:, 0:FIRST * TILES, :], x_view[:, 0:FIRST * TILES, :]).then_inc(x_first, 16)
            for layer in range(2):
                sp.dma_start(w_raw[:, layer, :, :], w["qkv_w"][layer]).then_inc(w_raw_in[layer], 16)
                sp.dma_start(b_qk[:, layer, :], w["qk_b"][layer]).then_inc(w_attn[layer], 16)
                sp.dma_start(b_v[:, layer:layer + 1], w["v_b"][layer]).then_inc(w_attn[layer], 16)
                sp.dma_start(w_out[:, layer, :], w["out_w"][layer]).then_inc(w_attn[layer], 16)
                sp.dma_start(b_out[:, layer, :], w["out_b"][layer].partition_broadcast(P)).then_inc(w_attn[layer], 16)
            sp.dma_start(X[:, FIRST * TILES:, :], x_view[:, FIRST * TILES:, :]).then_inc(x_rest, 16)
            for layer in range(2):
                sp.dma_start(gate_raw[:, layer, :], w["gate"][layer]).then_inc(w_gate_in, 16)
            sp.dma_start(b_up[:, :, :], w["b1"]).then_inc(w_gate_in, 16)
            sp.wait_ge(consts_dve, 1)
            sp.dma_start(b_down[0:EXPERTS, :], w["b2"]).then_inc(w_gate_in, 16)

            def load_up(dst, up, signal):
                sp.dma_start(dst[:, :, :], up.rearrange("e d h -> d e h")).then_inc(signal, 16)

            def load_down(layer):
                sp.dma_start(w_down[:, :, :, :], w["down"][layer].rearrange("e (c p) d -> p e c d", p=P)).then_inc(w_ffn_in, 16)
            sp.wait_ge(w_split, 2)
            load_up(raw_up, w["up"][0][0], up_in)
            load_down(0)
            load_up(raw_up2, w["up"][1][1][0:EXPERTS // 2], up2_in)

            for layer in range(2):
                base = layer * BATCHES

                def step(at):
                    b = at(0)
                    if b.exists:
                        after(sp, S["ks_ok"], b, 2, 2, base)
                        after(sp, S["st_ps"], at(RING), UNITS, UNITS, base)
                        if b.least == 0:
                            sp.wait_ge(kz_zero, 1)
                        for part in range(3):
                            for c in range(SLOTS):
                                row = 32 * part + HD * c
                                dst = kz[row:row + HD, b.ring, :, :].rearrange("p (g c) t -> p g c t", c=SLOTS)[:, :, c, :]
                                sp.dma_start(dst.bitcast(F32), k_stack[row:row + HD, b.ring, :, :].bitcast(F32))\
                                  .then_inc(kz_in[b.ring], 16)
                pipeline(sp, BATCHES, 4, step)

                if layer == 0:
                    sp.wait_ge(up_split, EXPERTS)
                    load_up(raw_up, w["up"][1][0], up_in)
                    sp.wait_ge(F["x_ok"], BATCHES * EXPERTS)
                    load_down(1)
                else:
                    sp.wait_ge(S["x_ok"], BATCHES * 2)
                    load_up(rest2, w["up"][1][1][EXPERTS // 2:], rest2_in)
            for b in range(0, BATCHES, 4):
                sp.wait_ge(F["x_ok"], EXPERTS * (BATCHES + b + 4))
                sp.dma_start(out_view[:, b * TILES:(b + 4) * TILES, :], X[:, b * TILES:(b + 4) * TILES, :]).then_inc(stored, 16)
            sp.wait_ge(stored, 16 * (BATCHES // 4))

        @block.gpsimd
        def _(pool):
            done = [0]

            def link(ins):
                done[0] += 1
                ins.then_inc(pool_chain, 1)
                pool.wait_ge(pool_chain, done[0])

            nc.gpsimd.memset(minus_half[:, :], -0.5)
            link(nc.gpsimd.memset(ident[:, :], 0.0))
            nc.gpsimd.affine_select(out=ident[:, :], in_=ident[:, :], compare_op=ALU.not_equal, fill=1.0,
                                    base=0, pattern=[[-1, P]], channel_multiplier=1).then_inc(masks_ok, 1)
            link(nc.gpsimd.memset(one_rows[:, :], 1.0))
            link(nc.gpsimd.affine_select(out=one_rows[:, :], in_=one_rows[:, :], compare_op=ALU.is_ge, fill=0.0,
                                         base=-96, pattern=[[-2, HEADS]], channel_multiplier=1))
            nc.gpsimd.affine_select(out=one_rows[:, :], in_=one_rows[:, :], compare_op=ALU.is_ge, fill=0.0,
                                    base=97, pattern=[[2, HEADS]], channel_multiplier=-1).then_inc(masks_ok, 1)
            pool.wait_ge(sel_zero, 1)
            for kind, parts in enumerate(((0, 1), (2,), (0, 2), (1,))):
                for part in parts:
                    for g in range(GROUPS):
                        view = sel_f[:, kind, g, 32 * part:32 * part + 32]
                        ins = nc.gpsimd.affine_select(out=view, in_=view, compare_op=ALU.not_equal, fill=1.0,
                                                      base=-32 * g, pattern=[[-1, 32]], channel_multiplier=1)
            ins.then_inc(sel_f_ok, 1)
            link(nc.gpsimd.memset(mask[:, :], 0.0))
            nc.gpsimd.affine_select(out=mask[:, :], in_=mask[:, :], compare_op=ALU.is_ge, fill=NEG,
                                    base=0, pattern=[[-1, P]], channel_multiplier=1).then_inc(masks_ok, 1)
            link(nc.gpsimd.memset(later[:, :, :], 1.0))
            nc.gpsimd.affine_select(out=later[:, 0, :], in_=later[:, 0, :], compare_op=ALU.is_gt, fill=0.0,
                                    base=0, pattern=[[-1, P]], channel_multiplier=1).then_inc(masks_ok, 1)
            link(nc.gpsimd.memset(floor1[:, :], FLOOR))
            nc.gpsimd.affine_select(out=floor1[:, :], in_=floor1[:, :], compare_op=ALU.not_equal, fill=3e38,
                                    base=-(P - 1), pattern=[[0, 1]], channel_multiplier=1).then_inc(masks_ok, 1)
            for r in range(RING):
                ins = nc.gpsimd.memset(kz[0:96, r, :, :].bitcast(F32), 0.0)
            ins.then_inc(kz_zero, 1)
            for layer in range(2):
                base = layer * BATCHES

                def rstd_of(b, M):
                    after(pool, M["ln_mv"], b, 1, 1, base)
                    ins = nc.gpsimd.tensor_tensor(rstd[:, :], var_eps[:, :], minus_half[:, :], ALU.pow)
                    if M is F:
                        ins.then_inc(F["rstd_ok"], 1)
                    else:
                        ins.then_inc(S["r_ok"], 1)
                        after(pool, S["r_ok"], b, 1, 1, base)
                        pool.sem_inc(pool_passed)
                        for t in range(TILES):
                            ins = nc.gpsimd.tensor_scalar(x_shift[:, t:t + 1], mv[:, t, 0:1], -1.0, rstd[:, t:t + 1], ALU.mult, ALU.mult)
                        ins.then_inc(S["rstd_ok"], 1)

                def select_unit(b, g, kind):
                    after(pool, S["p_exp"], b, UNITS, 3 * g + kind + 1, base)
                    pool.sem_inc(pool_passed)
                    view = probs[:, g, :, (kind - 1) * SEQ:(kind - 1) * SEQ + P]
                    nc.gpsimd.affine_select(out=view, in_=view, compare_op=ALU.is_ge, fill=0.0, base=0,
                                            pattern=[[0, SLOTS], [1, P]], channel_multiplier=-1).then_inc(S["p_sel"], 1)

                def step(at):
                    b0, b2, b3, b4 = at(0), at(2), at(3), at(4)
                    if b0.exists:
                        rstd_of(b0, S)
                    for slot in range(12):
                        if slot == 2 and b0.exists:
                            after(pool, S["xn_ok"], b0, 1, 1, base)
                            if b0.least == 0 and layer == 0:
                                pool.wait_ge(b_out_ok, 2)
                            nc.gpsimd.tensor_tensor(tiles(b0), tiles(b0), b_out[:, layer, :].unsqueeze(1).broadcast_to([P, TILES, D]),
                                                    ALU.add).then_inc(S["b_ok"], 1)
                        if slot == 2 and b4.exists:
                            after(pool, S["rd_ok"], b4, 1, 1, base)
                            nc.gpsimd.tensor_tensor(o_norm[:, :, :].rearrange("p t (h r) -> p (t h) r", r=HD), o_sum[:, :, :, :].rearrange("p a g r -> p (a g) r")[:, :, 0:HD],
                                                    o_rden[:, :].unsqueeze(2).broadcast_to([P, TILES * HEADS, HD]), ALU.mult).then_inc(S["o_norm_ok"], 1)
                        b, u = (b2, slot - 9) if slot >= 9 else (b3, slot + 3)
                        if b.exists and u % 3:
                            select_unit(b, u // 3, u % 3)
                pipeline(pool, BATCHES, 4, step)

                def fstep(at):
                    b0 = at(0)
                    if b0.exists:
                        rstd_of(b0, F)
                        after(pool, F["t_ok"], b0, 1, 1, base)
                        nc.gpsimd.tensor_tensor(gt["e"][:, :, :], base_e[:, :, :], gt["t"][:, :, :], ALU.pow).then_inc(F["e_ok"], 1)
                pipeline(pool, BATCHES, 2, fstep)

        @block.scalar
        def _(act):
            def norm_t_hi(b, M, base):
                after(act, M["t_ps"], b, 1, 1, base)
                nc.scalar.activation(xt_hi[:, b.ring, :], ps[:, BB if M is S else BTR, 0:SEQ], ACT.Copy).then_inc(M["xt_hi_ok"], 1)

            for layer in range(2):
                base = layer * BATCHES
                act.wait_ge(w_attn[layer], 64)
                if layer == 0:
                    act.wait_ge(consts_dve, 1)
                    act.wait_ge(masks_ok, 2)
                    for r in range(RING - 1):
                        ins = nc.scalar.activation(kz[96:P, r, :, :], one_rows[96:P, :].unsqueeze(2).broadcast_to([32, HEADS, SEQ]), ACT.Copy)
                    ins.then_inc(kz_ok, 1)

                def step(at):
                    b0, b1, b2, b3, b4 = (at(i) for i in range(5))
                    for slot in range(12):
                        b, u = (b2, slot - 9) if slot >= 9 else (b3, slot + 3)
                        if b.exists:
                            g, kind = u // 3, u % 3
                            after(act, S["st_ps"], b, UNITS, u + 1, base)
                            p = at(3) if slot >= 9 else at(4)
                            if kind == 0:
                                after(act, S["pv_ok"], p, GROUPS, g + 1, base)
                            dst = (probs[:, g, 0:2, 0:SEQ], probs[:, g, 2:4, 0:SEQ], probs[:, g, :, SEQ:3 * P])[kind]
                            nc.scalar.activation(dst, ps[:, BT[u % 2], :].rearrange("p (c q) -> p c q", q=SEQ if kind < 2 else P), ACT.Exp, scale=SCALE)\
                              .then_inc(S["p_exp"], 1)
                        if slot == 1 and b0.exists:
                            after(act, S["rstd_ok"], b0, 1, 1, base)
                            after(act, S["t_ps"], b1, 1, 1, base)
                            for t in range(TILES):
                                ins = nc.scalar.activation(xn[:, t, :], X[:, b0.number * TILES + t, :], ACT.Identity, bias=x_shift[:, t:t + 1], scale=rstd[:, t:t + 1])
                            ins.then_inc(S["xn_ok"], 1)
                        if slot == 0 and b4.exists:
                            after(act, S["pv_ok"], b4, GROUPS, GROUPS, base)
                            after(act, S["ot_ps"], at(5), 1, 1, base)
                            nc.scalar.activation(o_rows[:, :, :].rearrange("p a t -> p (a t)"), ps[:, BO, :], ACT.Copy)\
                              .then_inc(S["o_rows_ok"], 1)
                        if slot == 2 and b1.exists:
                            after(act, S["v_ps"], b1, 1, 1, base)
                            after(act, S["pv_ok"], b4, GROUPS, GROUPS, base)
                            for t in range(TILES):
                                ins = nc.scalar.activation(v_view(b1.ring, t, HD), ps[:, BB, t * P:(t + 1) * P].rearrange("p (g c r) -> p g c r", g=GROUPS, c=SLOTS), ACT.Copy)
                            ins.then_inc(S["v_ok"], 1)
                        if slot == 2 and b4.exists and layer == 1:
                            after(act, S["ot_ps"], b4, 1, 1, base)
                            nc.scalar.activation(o_sum[:, :, 0:3, :], ps[:, BR, 0:SEQ].rearrange("p (a b) -> p a b", b=32)[:, :, 0:27].rearrange("p a (g r) -> p a g r", g=3), ACT.Copy)
                            nc.scalar.activation(o_sum[:, :, 3, :], ps[:, BR, SEQ:2 * SEQ].rearrange("p (a b) -> p a b", b=32)[:, :, 0:HD + 1], ACT.Copy)\
                              .then_inc(S["os_ok"], 1)
                        if slot == 5 and b4.exists:
                            after(act, S["t2_ps"], b4, 1, 1, base)
                            nc.scalar.activation(o_t[:, :], ps[:, BR, 0:SEQ], ACT.Copy).then_inc(S["o_t_ok"], 1)
                        if slot == 3 and b0.exists:
                            norm_t_hi(b0, S, base)
                        if slot == 5 and b0.exists:
                            after(act, S["qk_ps"], b0, 1, 1, base)
                            for t in range(2):
                                ins = nc.scalar.activation(qk_hi[:, t, :], ps[:, BA, t * SEQ:(t + 1) * SEQ], ACT.Identity, bias=b_qk[:, layer, t:t + 1])
                            ins.then_inc(S["qk_hi_ok"], 1)
                        if slot in (8, 9, 10, 11) and b0.exists:
                            e = (8, 9, 10, 11).index(slot)
                            after(act, S["e_ps"], b0, 4, e + 1, base)
                            dst = (k_stack if e < 2 else q_stack)[:, b0.ring, 2 * (e % 2):2 * (e % 2) + 2, :]
                            if e == 0:
                                p = at(RING)
                                if p.exists:
                                    act.wait_ge(kz_in[p.ring], (p.turn + (layer * TURNS[p.ring] + 1)) * 192)
                            if e == 2:
                                after(act, S["st_ps"], at(RING), UNITS, UNITS, base)
                            nc.scalar.activation(dst, ps[:, BA if e % 2 == 0 else BB, :].rearrange("p (g t) -> p g t", g=2), ACT.Copy)\
                              .then_inc(S["ks_ok" if e < 2 else "qs_ok"], 1)
                        if slot == 7 and b2.exists:
                            after(act, S["mt_ps"], b2, 1, 1, base)
                            after(act, S["s_ps"], b2, UNITS, UNITS, base)
                            nc.scalar.activation(q_stack[96:P, b2.ring, :, :], ps[96:P, BB, 0:SEQ].unsqueeze(1).broadcast_to([32, GROUPS, SEQ]), ACT.Copy)\
                              .then_inc(S["m_rep"], 1)
                            if layer == 0:
                                after(act, S["cu_ok"], at(2 + RING), 1, 1, base)
                                nc.scalar.activation(c_fill[:, b2.ring, :, :], neg_m[:, b2.ring, :, :], ACT.Exp, bias=fill_bias[:, :], scale=SCALE)\
                                  .then_inc(S["c_ok"], 1)
                pipeline(act, BATCHES, 4, step)

                def fstep(at):
                    b0, b1, b2 = at(0), at(1), at(2)
                    for slot in range(8):
                        if slot == 2 and b0.exists:
                            norm_t_hi(b0, F, base)
                        if slot == 3 and b1.exists and layer == 0:
                            after(act, F["gt_ps"], b1, 1, 1, base)
                            after(act, F["y9_ps"], b2, 1, 1, base)
                            nc.scalar.activation(g_rows[:, :], ps[:, BG, 0:SEQ], ACT.Copy).then_inc(F["gr_ok"], 1)
                        if b1.exists:
                            e = slot
                            after(act, F["up_ps"], b1, EXPERTS, e + 1, base)
                            if layer == 0:
                                if e >= HIDS:
                                    after(act, F["y_ps"], b1, EXPERTS, e - HIDS + 1, base)
                                else:
                                    after(act, F["y_ps"], b2, EXPERTS, EXPERTS - HIDS + 1 + e, base)
                                for ch in range(CHUNKS):
                                    ins = nc.scalar.activation(hid[:, e % HIDS, ch, :], ps[:, U0[e % 2], ch * SEQ:(ch + 1) * SEQ], ACT.Relu, bias=b_up[:, e, ch:ch + 1])
                                ins.then_inc(F["hid_ok"], 1)
                            else:
                                if e >= 2:
                                    after(act, F["hid_ok"], b1, EXPERTS, e - 1, base)
                                else:
                                    after(act, F["hid_ok"], at(2), EXPERTS, EXPERTS - 1 + e, base)
                                nc.scalar.activation(silu[:, e % 2, :, :].rearrange("p c t -> p (c t)"), ps[:, U0[e % 2], :], ACT.Silu).then_inc(F["silu_ok"], 1)
                act.wait_ge(w_gate_in, 64)
                act.wait_ge(S["x_ok"], BATCHES * (layer + 1))
                for e in range(EXPERTS):
                    if e == 0:
                        act.wait_ge(up_in, 16 * (layer + 1))
                        if layer:
                            act.wait_ge(up2_in, 16)
                    if e == EXPERTS // 2 and layer:
                        act.wait_ge(rest2_in, 16)
                    for k in range(1 + layer):
                        nc.scalar.activation(up_w(k, 0, e), up_raw(k, e), ACT.Copy).then_inc(up_hi, 1)
                pipeline(act, BATCHES, 2, fstep)

        @block.tensor
        def _(pe):
            for layer in range(2):
                pe.wait_ge(w_attn[layer], 64)
                pe.wait_ge(b_v_wide, layer + 1)
                nc.tensor.matmul(ps[:, BR, layer * D:(layer + 1) * D], o_norm[:, layer, :], w_out[:, layer, :], start=True, stop=True, skip_group_check=True).then_inc(b_v_ps, 1)
            for layer in range(2):
                base = layer * BATCHES
                pe.wait_ge(w_attn[layer], 64)
                pe.wait_ge(consts_dve, 1)

                def turn_norm(b, M, bank):
                    after(pe, M["xn_ok"], b, 1, 1, base)
                    if b.least == 0 and M is S and layer == 0:
                        pe.wait_ge(masks_ok, 1)
                    for t in range(TILES):
                        ins = nc.tensor.transpose(ps[:, bank, t * P:(t + 1) * P], xn[:, t, :], ident[:, :])
                    ins.then_inc(M["t_ps"], 1)

                def step(at):
                    b0, b1, b2, b3, b4 = (at(i) for i in range(5))
                    for slot in range(12):
                        b, u = (b1, slot - 6) if slot >= 6 else (b2, slot + 6)
                        if b.exists:
                            g, kind = u // 3, u % 3
                            qt, kt = (0, 1, 1)[kind], (0, 0, 1)[kind]
                            if u == 0:
                                if b.least == 0 and layer == 0:
                                    pe.wait_ge(kz_ok, 2)
                                pe.wait_ge(kz_in[b.ring], (b.turn + (layer * TURNS[b.ring] + 1)) * 192)
                                after(pe, S["qs_ok"], b, 2, 2, base)
                            if u >= 2:
                                after(pe, S["s_max"], b, UNITS, u - 1, base)
                            else:
                                after(pe, S["s_max"], at(2), UNITS, UNITS - 1 + u, base)
                            bank = ps[:, BS[u % 2], :]
                            nc.tensor.matmul(bank, q_stack[:, b.ring, g, qt * P:(qt + 1) * P], kz[:, b.ring, g * SLOTS:(g + 1) * SLOTS, kt * P:(kt + 1) * P],
                                             start=True, stop=True, skip_group_check=True).then_inc(S["s_ps"], 1)
                        if slot == 7 and b2.exists:
                            after(pe, S["m_ok"], b2, 1, 1, base)
                            after(pe, S["xt_lo_ok"], b0, 1, 1, base)
                            for t in range(TILES):
                                ins = nc.tensor.transpose(ps[:, BB, t * P:(t + 1) * P], m_pad[:, t, :].bitcast(F32), ident[:, :])
                            ins.then_inc(S["mt_ps"], 1)
                        b, u = (b2, slot - 9) if slot >= 9 else (b3, slot + 3)
                        if b.exists:
                            g, kind = u // 3, u % 3
                            if u == 0:
                                after(pe, S["m_rep"], b, 1, 1, base)
                            if u >= 2:
                                after(pe, S["p_exp"], b, UNITS, u - 1, base)
                            else:
                                after(pe, S["p_exp"], at(3), UNITS, UNITS - 1 + u, base)
                            heads, kt = (range(2), range(2, 4), range(4))[kind], kind // 2
                            for j, c in enumerate(heads):
                                n = SEQ - kt * P
                                ins = nc.tensor.matmul(ps[:, BT[u % 2], j * n:(j + 1) * n], kz[:, b.ring, g * SLOTS + c, kt * P:(kt + 1) * P],
                                                       q_stack[:, b.ring, g, kt * P:], start=True, stop=True, skip_group_check=True)
                            ins.then_inc(S["st_ps"], 1)
                        if slot in (2, 5, 8, 11) and b3.exists:
                            g = (slot - 2) // 3
                            after(pe, S["p_sel"], b3, 2 * GROUPS, 2 * g + 2, base)
                            if g == 0:
                                after(pe, S["v_ok"], b3, 1, 1, base)
                                after(pe, S["o_rows_ok"], b4, 1, 1, base)
                            col = 0 if g < 3 else SEQ
                            for kt in range(TILES):
                                for c in range(SLOTS):
                                    lo = g * P + c * VC if g < 3 else 3 * VG + c * VC
                                    ins = nc.tensor.matmul(ps[32 * c:32 * c + 32, BO, col + kt * P:col + SEQ], v_pad[:, b3.ring, kt, lo:lo + 32],
                                                           probs[:, g, c, 0:SEQ] if kt == 0 else probs[:, g, c, SEQ:3 * P],
                                                           start=(kt == 0 and g in (0, 3)), stop=(kt == 1), skip_group_check=True)
                            ins.then_inc(S["pv_ok"], 1)
                        if slot == 1 and b4.exists:
                            after(pe, S["o_rows_ok"], b4, 1, 1, base)
                            after(pe, S["x_ok"], at(5), 1, 1, base)
                            for half in range(2):
                                for t in range(TILES):
                                    ins = nc.tensor.transpose(ps[:, BR, (2 * half + t) * P:(2 * half + t + 1) * P], o_rows[:, half, t * P:(t + 1) * P], ident[:, :])
                            ins.then_inc(S["ot_ps"], 1)
                        if slot == 4 and b4.exists:
                            after(pe, S["o_norm_ok"], b4, 1, 1, base)
                            for t in range(TILES):
                                ins = nc.tensor.transpose(ps[:, BR, t * P:(t + 1) * P], o_norm[:, t, :], ident[:, :])
                            ins.then_inc(S["t2_ps"], 1)
                        if slot == 6 and b4.exists:
                            after(pe, S["o_t_ok"], b4, 1, 1, base)
                            for t in range(TILES):
                                ins = nc.tensor.matmul(ps[:, BR, SEQ + t * P:SEQ + (t + 1) * P], o_t[:, t * P:(t + 1) * P], w_out[:, layer, :], start=True, stop=True, skip_group_check=True)
                            ins.then_inc(S["y_ps"], 1)
                        if slot == 1 and b1.exists:
                            after(pe, S["qs_ok"], b1, 2, 2, base)
                            after(pe, S["xt_lo_ok"], b1, 1, 1, base)
                            for t in range(TILES):
                                for j, (a, ww) in enumerate(((xt_hi, w_hi), (xt_lo, w_hi), (xt_hi, w_lo))):
                                    ins = nc.tensor.matmul(ps[:, BB, t * P:(t + 1) * P], a[:, b1.ring, t * P:(t + 1) * P], ww[:, layer, 2, :], start=(j == 0), stop=(j == 2), skip_group_check=True)
                            ins.then_inc(S["v_ps"], 1)
                        if slot == 3 and b0.exists:
                            after(pe, S["v_ok"], b1, 1, 1, base)
                            turn_norm(b0, S, BB)
                        if slot == 5 and b0.exists:
                            after(pe, S["xt_lo_ok"], b0, 1, 1, base)
                            if b0.least == 0:
                                pe.wait_ge(w_split, 2)
                            after(pe, S["qs_ok"], b1, 2, 2, base)
                            if layer == 0:
                                after(pe, S["cu_ok"], b3, 1, 1, base)
                            for t in range(2):
                                for j, (a, ww) in enumerate(((xt_hi, w_hi), (xt_lo, w_hi), (xt_hi, w_lo))):
                                    ins = nc.tensor.matmul(ps[:, BA, t * SEQ:(t + 1) * SEQ], ww[:, layer, t, :], a[:, b0.ring, :], start=(j == 0), stop=(j == 2), skip_group_check=True)
                            ins.then_inc(S["qk_ps"], 1)
                        if slot in (8, 9, 10, 11) and b0.exists:
                            e = (8, 9, 10, 11).index(slot)
                            if e == 0:
                                after(pe, S["qk_lo_ok"], b0, 1, 1, base)
                                if b0.least == 0 and layer == 0:
                                    pe.wait_ge(sel_ok, 1)
                            if e == 1:
                                after(pe, S["m_rep"], b2, 1, 1, base)
                                if not b2.exists:
                                    after(pe, S["xt_lo_ok"], b0, 1, 1, base)
                            if e >= 2:
                                after(pe, S["ks_ok"], b0, 2, e - 1, base)
                            t = 1 if e < 2 else 0
                            for g2 in range(2):
                                g = 2 * (e % 2) + g2
                                for part, src in enumerate((qk_hi, qk_lo)):
                                    ins = nc.tensor.matmul(ps[:, BA if e % 2 == 0 else BB, g2 * SEQ:(g2 + 1) * SEQ], sel[:, 2 * (e >= 2) + part, g, :], src[:, t, :],
                                                           start=(part == 0), stop=(part == 1), skip_group_check=True)
                            ins.then_inc(S["e_ps"], 1)
                        if slot == 0 and b3.exists and layer == 0:
                            if b3.least == 0:
                                pe.wait_ge(masks_ok, 5)
                            after(pe, S["v_ok"], b3, 1, 1, base)
                            after(pe, S["qs_ok"], b1, 2, 1, base)
                            for t, kt, m, first in ((0, 0, 0, True), (0, 1, 1, False), (1, 1, 0, True)):
                                vv = v_view(b3.ring, kt, HD + 1)
                                ins = nc.tensor.matmul(ps[:, BA, t * 144:(t + 1) * 144], later[:, m, :], vv, start=first, stop=(kt == 1), skip_group_check=True)
                            ins.then_inc(S["u_ps"], 1)
                pipeline(pe, BATCHES, 4, step)

                pe.wait_ge(S["x_ok"], BATCHES * (layer + 1))
                pe.wait_ge(w_ffn_in, 16 * (layer + 1))
                pe.wait_ge(w_gate_in, 64)
                pe.wait_ge(w_split, 3)
                ups = 1 if layer == 0 else 2

                def fstep(at):
                    b0, b1, b2 = at(0), at(1), at(2)
                    for slot in range(8):
                        if slot == 2 and b1.exists and layer == 0:
                            after(pe, F["g_ok"], b1, 1, 1, base)
                            for t in range(TILES):
                                ins = nc.tensor.transpose(ps[:, BG, t * P:(t + 1) * P], g_pad[:, b1.ring, t, :], ident[:, :])
                            ins.then_inc(F["gt_ps"], 1)
                        if slot == 4 and b1.exists and layer == 0:
                            after(pe, F["gr_ok"], b1, 1, 1, base)
                            after(pe, F["y9_ok"], b2, 1, 1, base)
                            for t in range(TILES):
                                ins = nc.tensor.matmul(ps[:, BG, SEQ + t * P:SEQ + (t + 1) * P], g_rows[:, t * P:(t + 1) * P], b_down[:, :], start=True, stop=True, skip_group_check=True)
                            ins.then_inc(F["y9_ps"], 1)
                        if b1.exists:
                            e = slot
                            if e == 0:
                                after(pe, F["xt_lo_ok"], b1, 1, 1, base)
                            if b1.least == 0:
                                pe.wait_ge(up_split, EXPERTS * layer + ups * (e + 1))
                            free = F["hid_ok"]
                            if e >= 2:
                                after(pe, free, b1, EXPERTS, e - 1, base)
                            else:
                                after(pe, free, at(2), EXPERTS, EXPERTS - 1 + e, base)
                            for k in range(ups):
                                bank = (U0, U1)[k][e % 2]
                                for ch in range(CHUNKS):
                                    for j, (a, part) in enumerate(((xt_hi, 0), (xt_lo, 0), (xt_hi, 1))):
                                        ins = nc.tensor.matmul(ps[:, bank, ch * SEQ:(ch + 1) * SEQ], up_w(k, part, e)[:, ch * P:(ch + 1) * P], a[:, b1.ring, :], start=(j == 0), stop=(j == 2), skip_group_check=True)
                            ins.then_inc(F["up_ps"], 1)
                        b, e = (b1, slot - 2) if slot >= 2 else (b2, slot + EXPERTS - 2)
                        if b.exists:
                            after(pe, F["hid_ok"], b, EXPERTS, e + 1, base)
                            if e >= 2:
                                after(pe, F["x_ok"], b, EXPERTS, e - 1, base)
                            else:
                                after(pe, F["x_ok"], b2, EXPERTS, EXPERTS - 1 + e, base)
                            for t in range(TILES):
                                for ch in range(CHUNKS):
                                    ins = nc.tensor.matmul(ps[:, BY[e % 2], t * P:(t + 1) * P], hid[:, e % HIDS, ch, t * P:(t + 1) * P], w_down[:, e, ch, :], start=(ch == 0), stop=(ch == 1), skip_group_check=True)
                            ins.then_inc(F["y_ps"], 1)
                        if slot == 2 and b0.exists:
                            after(pe, F["xt_lo_ok"], b1, 1, 1, base)
                            turn_norm(b0, F, BTR)
                        if slot == 4 and b0.exists:
                            after(pe, F["xt_lo_ok"], b0, 1, 1, base)
                            if layer == 0:
                                after(pe, F["gr_ok"], b1, 1, 1, base)
                            else:
                                after(pe, F["t_ok"], b1, 1, 1, base)
                            for t in range(TILES):
                                for j, (a, ww) in enumerate(((xt_hi, gate_hi), (xt_lo, gate_hi), (xt_hi, gate_lo))):
                                    ins = nc.tensor.matmul(ps[:, BG, t * EXPERTS:(t + 1) * EXPERTS], a[:, b0.ring, t * P:(t + 1) * P], ww[:, layer, :], start=(j == 0), stop=(j == 2), skip_group_check=True)
                            ins.then_inc(F["lg_ps"], 1)
                pipeline(pe, BATCHES, 2, fstep)

        @block.vector
        def _(dve):
            nc.vector.memset(sel_f, 0.0).then_inc(sel_zero, 1)
            for r in range(RING):
                nc.vector.memset(v_pad[:, r, :, :], 0.0)
                nc.vector.memset(g_pad[:, r, :, :], 0.0)
            nc.vector.memset(m_pad[:, :, :].bitcast(F32), 0.0)
            nc.vector.memset(fill_bias[:, :], FILL)
            nc.vector.memset(base_e[:, :, :], 2.718281828459045)
            for e in range(EXPERTS):
                nc.vector.memset(rank[:, :, e], float(EXPERTS - e))
            nc.vector.memset(b_down[:, :], 0.0).then_inc(dve_chain, 1)
            dve.wait_ge(dve_chain, 1)
            for r in range(RING):
                for g in range(GROUPS):
                    at = g * VG + HD
                    ins = nc.vector.memset(v_pad[:, r, :, at:at + 3 * VC + 1:VC], 1.0)
            ins.then_inc(consts_dve, 1)
            chain = [1]

            def link(ins):
                chain[0] += 1
                ins.then_inc(dve_chain, 1)
                dve.wait_ge(dve_chain, chain[0])

            for layer in range(2):
                dve.wait_ge(w_attn[layer], 64)
                nc.vector.tensor_copy(o_norm[:, layer, :], b_v[:, layer:layer + 1].broadcast_to([P, D])).then_inc(b_v_wide, 1)
                dve.wait_ge(w_raw_in[layer], 16)
                link(nc.vector.tensor_copy(w_hi[:, layer, :, :], w_raw[:, layer, :, :]))
                nc.vector.tensor_tensor(w_lo[:, layer, :, :], w_raw[:, layer, :, :], w_hi[:, layer, :, :].bitcast(F32), ALU.subtract).then_inc(w_split, 1)
            dve.wait_ge(b_v_ps, 2)
            for layer in range(2):
                nc.vector.tensor_tensor(b_out[:, layer, :], b_out[:, layer, :], ps[:, BR, layer * D:(layer + 1) * D], ALU.add).then_inc(b_out_ok, 1)
            dve.wait_ge(masks_ok, 2)
            nc.vector.tensor_copy(kz[96:P, RING - 1, :, :], one_rows[96:P, :].unsqueeze(2).broadcast_to([32, HEADS, SEQ])).then_inc(kz_ok, 1)
            dve.wait_ge(sel_f_ok, 1)
            nc.vector.tensor_copy(sel[:, :, :, :], sel_f).then_inc(sel_ok, 1)

            for layer in range(2):
                base = layer * BATCHES

                dve.wait_ge(w_attn[layer], 64)
                if layer:
                    dve.wait_ge(F["x_ok"], BATCHES * EXPERTS)

                def stats_of(b, M):
                    for t in range(TILES):
                        ins = nc.vector.bn_stats(stats[:, t, :], one_tile(b, t))
                    ins.then_inc(M["st_ok"], 1)
                    after(dve, M["st_ok"], b, 1, 1, base)
                    dve.sem_inc(dve_passed)
                    for t in range(TILES):
                        ins = nc.vector.bn_aggr(mv[:, t, :], stats[:, t, :])
                    ins.then_inc(M["ag_ok"], 1)
                    after(dve, M["ag_ok"], b, 1, 1, base)
                    nc.vector.tensor_scalar(var_eps[:, :], mv[:, :, 1], EPS, None, ALU.add).then_inc(M["ln_mv"], 1)

                def norm_of(b):
                    after(dve, F["rstd_ok"], b, 1, 1, base)
                    for t in range(TILES):
                        ins = nc.vector.tensor_scalar(xn[:, t, :], one_tile(b, t), mv[:, t, 0:1], rstd[:, t:t + 1], ALU.subtract, ALU.mult)
                    ins.then_inc(F["xn_ok"], 1)

                def norm_t_lo(b, M):
                    after(dve, M["xt_hi_ok"], b, 1, 1, base)
                    nc.vector.tensor_tensor(xt_lo[:, b.ring, :], ps[:, BB if M is S else BTR, 0:SEQ], xt_hi[:, b.ring, :].bitcast(F32), ALU.subtract).then_inc(M["xt_lo_ok"], 1)

                def step(at):
                    b0, b1, b2, b3, b4 = (at(i) for i in range(5))
                    for slot in range(12):
                        if slot == 0 and b0.exists:
                            if layer == 0 and b0.least == 0:
                                dve.wait_ge(x_first, 16)
                            if layer == 0 and b0.least == FIRST:
                                dve.wait_ge(x_rest, 16)
                            stats_of(b0, S)
                        if slot == 1 and b3.exists and layer == 0:
                            after(dve, S["u_ps"], b3, 1, 1, base)
                            after(dve, S["c_ok"], b3, 1, 1, base)
                            for t in range(TILES):
                                out = c_u[:, b3.ring, t * SLOTS:(t + 1) * SLOTS, :, :]
                                ins = nc.vector.tensor_tensor(out, ps[:, BA, t * 144:(t + 1) * 144].rearrange("p (g c r) -> p c g r", g=GROUPS, c=SLOTS),
                                                              c_fill[:, b3.ring, t, :].rearrange("p (g c) -> p c g", g=GROUPS).unsqueeze(3).broadcast_to([P, SLOTS, GROUPS, HD + 1]), ALU.mult)
                            ins.then_inc(S["cu_ok"], 1)
                        if slot == 6 and b2.exists:
                            nm, m = neg_max[:, b2.ring, :, :], neg_m[:, b2.ring, :, :]
                            after(dve, S["s_max"], b2, UNITS, UNITS, base)
                            if layer == 0:
                                after(dve, S["c_ok"], at(2 + RING), 1, 1, base)
                                nc.vector.tensor_scalar(m[:, 0, :], nm[:, 0, :], FLOOR, None, ALU.min)
                                nc.vector.scalar_tensor_tensor(out=m[:, 1, :], in0=nm[:, 1, :], scalar=floor1[:, 0:1], in1=nm[:, 2, :], op0=ALU.min, op1=ALU.min).then_inc(S["nm_ok"], 1)
                            else:
                                nc.vector.tensor_copy(m[:, 0, :], nm[:, 0, :])
                                nc.vector.tensor_tensor(m[:, 1, :], nm[:, 1, :], nm[:, 2, :], ALU.min).then_inc(S["nm_ok"], 1)
                            after(dve, S["nm_ok"], b2, 1, 1, base)
                            after(dve, S["mt_ps"], at(3), 1, 1, base)
                            nc.vector.tensor_copy(m_pad[:, :, 96:P:2], m).then_inc(S["mh_ok"], 1)
                            after(dve, S["mh_ok"], b2, 1, 1, base)
                            nc.vector.tensor_tensor(m_pad[:, :, 97:P:2], m, m_pad[:, :, 96:P:2].bitcast(F32), ALU.subtract).then_inc(S["m_ok"], 1)
                        if slot == 7 and b0.exists:
                            after(dve, S["qk_hi_ok"], b0, 1, 1, base)
                            for t in range(2):
                                ins = nc.vector.scalar_tensor_tensor(out=qk_lo[:, t, :], in0=ps[:, BA, t * SEQ:(t + 1) * SEQ], scalar=b_qk[:, layer, t:t + 1],
                                                                     in1=qk_hi[:, t, :].bitcast(F32), op0=ALU.add, op1=ALU.subtract)
                            ins.then_inc(S["qk_lo_ok"], 1)
                        b, u = (b1, slot - 6) if slot >= 6 else (b2, slot + 6)
                        if b.exists:
                            g, kind = u // 3, u % 3
                            if u == 0 and b.least == 0 and layer == 0:
                                dve.wait_ge(masks_ok, 5)
                            after(dve, S["s_ps"], b, UNITS, u + 1, base)
                            if kind == 1:
                                nc.vector.tensor_reduce(neg_max[:, b.ring, kind, g * SLOTS:(g + 1) * SLOTS], ps[:, BS[u % 2], :].rearrange("p (c k) -> p c k", c=SLOTS),
                                                        AX.X, ALU.max, negate=True).then_inc(S["s_max"], 1)
                            else:
                                dve.sem_inc(dve_passed)
                                for c in range(SLOTS):
                                    ins = nc.vector.tensor_tensor_reduce(out=ps[:, BS[u % 2], c * P:(c + 1) * P], in0=ps[:, BS[u % 2], c * P:(c + 1) * P], in1=mask[:, :], scale=-1.0, scalar=3e38,
                                                                         op0=ALU.add, op1=ALU.min, accum_out=neg_max[:, b.ring, kind, g * SLOTS + c:g * SLOTS + c + 1])
                                ins.then_inc(S["s_max"], 1)
                        if slot == 2 and b4.exists:
                            after(dve, S["ot_ps"], b4, 1, 1, base)
                            if layer == 0:
                                for part, gg in ((0, slice(0, 3)), (1, slice(3, 4))):
                                    src = ps[:, BR, part * SEQ:(part + 1) * SEQ].rearrange("p (a b) -> p a b", b=32)[:, :, 0:9 * (3 if part == 0 else 1)]
                                    ins = nc.vector.tensor_tensor(o_sum[:, :, gg, :].rearrange("p a g r -> p a (g r)"), src, c_u[:, b4.ring, :, gg, :].rearrange("p a g r -> p a (g r)"), ALU.add)
                                ins.then_inc(S["os_ok"], 1)
                            after(dve, S["os_ok"], b4, 1, 1, base)
                            nc.vector.reciprocal(o_rden[:, :], o_sum[:, :, :, :].rearrange("p a g r -> p (a g) r")[:, :, HD]).then_inc(S["rd_ok"], 1)
                        if slot == 4 and b0.exists:
                            norm_t_lo(b0, S)
                        if slot == 8 and b4.exists:
                            after(dve, S["y_ps"], b4, 1, 1, base)
                            after(dve, S["b_ok"], b4, 1, 1, base)
                            nc.vector.tensor_tensor(tiles(b4), tiles(b4), ps[:, BR, SEQ:2 * SEQ].rearrange("p (t d) -> p t d", t=TILES), ALU.add).then_inc(S["x_ok"], 1)
                pipeline(dve, BATCHES, 4, step)

                if layer == 0:
                    dve.wait_ge(w_gate_in, 64)
                    link(nc.vector.tensor_copy(gate_hi[:, :, :], gate_raw[:, :, :]))
                    nc.vector.tensor_tensor(gate_lo[:, :, :], gate_raw[:, :, :], gate_hi[:, :, :].bitcast(F32), ALU.subtract).then_inc(w_split, 1)
                dve.wait_ge(S["x_ok"], BATCHES * (layer + 1))
                for e in range(EXPERTS):
                    for k in range(1 + layer):
                        dve.wait_ge(up_hi, EXPERTS * layer + e * (1 + layer) + k + 1)
                        nc.vector.tensor_tensor(up_w(k, 1, e), up_raw(k, e), up_w(k, 0, e).bitcast(F32), ALU.subtract).then_inc(up_split, 1)

                def fstep(at):
                    b0, b1, b2 = at(0), at(1), at(2)
                    for slot in range(8):
                        b, e = (b1, slot - 3) if slot >= 3 else (b2, slot + EXPERTS - 3)
                        if b.exists:
                            after(dve, F["y_ps"], b, EXPERTS, e + 1, base)
                            after(dve, *((F["x_ok"], b, EXPERTS, e) if e else (F["g_ok"], b, 1, 1)), base)
                            for t in range(TILES):
                                ins = nc.vector.scalar_tensor_tensor(out=one_tile(b, t), in0=ps[:, BY[e % 2], t * P:(t + 1) * P], scalar=g_pad[:, b.ring, t, e:e + 1],
                                                                     in1=one_tile(b, t), op0=ALU.mult, op1=ALU.add)
                            ins.then_inc(F["x_ok"], 1)
                        if slot == 6 and b1.exists and layer == 0:
                            after(dve, F["y9_ps"], b1, 1, 1, base)
                            after(dve, F["x_ok"], b1, EXPERTS, e + 1, base)
                            nc.vector.tensor_tensor(tiles(b1), tiles(b1), ps[:, BG, SEQ:2 * SEQ].rearrange("p (t d) -> p t d", t=TILES), ALU.add).then_inc(F["y9_ok"], 1)
                            after(dve, F["y9_ok"], b1, 1, 1, base)
                        if b1.exists and layer == 1:
                            e = slot
                            after(dve, F["silu_ok"], b1, EXPERTS, e + 1, 0)
                            if e >= HIDS:
                                after(dve, F["y_ps"], b1, EXPERTS, e - HIDS + 1, base)
                            else:
                                after(dve, F["y_ps"], b2, EXPERTS, EXPERTS - HIDS + 1 + e, base)
                            nc.vector.tensor_tensor(hid[:, e % HIDS, :, :].rearrange("p c t -> p (c t)"), silu[:, e % 2, :, :].rearrange("p c t -> p (c t)"), ps[:, U1[e % 2], :], ALU.mult).then_inc(F["hid_ok"], 1)
                        if slot == 0 and b0.exists:
                            stats_of(b0, F)
                        if slot == 1 and b0.exists:
                            after(dve, F["t_ps"], b1, 1, 1, base)
                            norm_of(b0)
                        if slot == 3 and b0.exists:
                            norm_t_lo(b0, F)
                        if slot >= 5 and b0.exists:
                            top_two(b0, slot - 5)

                def top_two(b, part):
                    count = [(0, 5, 11)[part]]

                    def chained(ins):
                        count[0] += 1
                        ins.then_inc(F["top"], 1)
                        after(dve, F["top"], b, TOP, count[0], base)

                    def wide(s):
                        return s[:, :].unsqueeze(2).broadcast_to([P, TILES, EXPERTS])

                    def first_of(hot, key, mk, se):
                        chained(nc.vector.tensor_tensor(gt[key][:, :, :], gt[hot][:, :, :], rank[:, :, :], ALU.mult))
                        chained(nc.vector.tensor_reduce(gs[mk][:, :], gt[key][:, :, :], AX.X, ALU.max))
                        chained(nc.vector.tensor_tensor(gt[se][:, :, :], gt[key][:, :, :], wide(gs[mk]), ALU.is_equal))

                    if part == 0:
                        logits = ps[:, BG, 0:TILES * EXPERTS].rearrange("p (t e) -> p t e", t=TILES)
                        after(dve, F["lg_ps"], b, 1, 1, base)
                        chained(nc.vector.tensor_reduce(gs["v1"][:, :], logits, AX.X, ALU.max))
                        nc.vector.tensor_tensor(gt["t"][:, :, :], logits, wide(gs["v1"]), ALU.subtract).then_inc(F["t_ok"], 1)
                        after(dve, F["t_ok"], b, 1, 1, base)
                        chained(nc.vector.tensor_scalar(gt["hot"][:, :, :], gt["t"][:, :, :], 0.0, None, ALU.is_ge))
                        first_of("hot", "key", "mk1", "sel1")
                    elif part == 1:
                        chained(nc.vector.scalar_tensor_tensor(out=gt["t2"][:, :, :], in0=gt["sel1"][:, :, :], scalar=-3e38, in1=gt["t"][:, :, :], op0=ALU.mult, op1=ALU.add))
                        chained(nc.vector.tensor_reduce(gs["v2"][:, :], gt["t2"][:, :, :], AX.X, ALU.max))
                        chained(nc.vector.tensor_tensor(gt["hot2"][:, :, :], gt["t2"][:, :, :], wide(gs["v2"]), ALU.is_ge))
                        first_of("hot2", "key2", "mk2", "sel2")
                    else:
                        chained(nc.vector.tensor_tensor(gt["both"][:, :, :], gt["sel1"][:, :, :], gt["sel2"][:, :, :], ALU.add))
                        after(dve, F["e_ok"], b, 1, 1, base)
                        chained(nc.vector.tensor_tensor(gt["we"][:, :, :], gt["both"][:, :, :], gt["e"][:, :, :], ALU.mult))
                        chained(nc.vector.tensor_reduce(gs["sum"][:, :], gt["we"][:, :, :], AX.X, ALU.add))
                        chained(nc.vector.reciprocal(gs["rsum"][:, :], gs["sum"][:, :]))
                        assert count[0] == TOP
                        nc.vector.tensor_tensor(g_pad[:, b.ring, :, 0:EXPERTS], gt["we"][:, :, :], wide(gs["rsum"]), ALU.mult).then_inc(F["g_ok"], 1)
                pipeline(dve, BATCHES, 2, fstep)


def kernel(**inputs):
    import numpy as _np
    import concourse.bacc as _bacc
    from concourse.bass_utils import run_bass_kernel_spmd as _run

    nc = _bacc.Bacc("TRN2", target_bir_lowering=False, num_devices=1)
    arrays = {}

    def dram(name, a):
        a = _np.ascontiguousarray(a)
        arrays[name] = a
        return nc.dram_tensor(name, a.shape, mybir.dt.from_np(a.dtype), kind="ExternalInput").ap()

    i = {k: _np.asarray(v) for k, v in inputs.items()}
    w0, w1 = i["L0_attn_attn_W"], i["L1_attn_qkv_w"]
    b0, b1 = i["L0_attn_attn_b"], i["L1_attn_qkv_b"]
    qkv_b = (b0.reshape(SLOTS, GROUPS, 3, HD).transpose(2, 1, 0, 3).reshape(3, D),
             b1.reshape(3, SLOTS, GROUPS, HD).transpose(0, 2, 1, 3).reshape(3, D))
    w = {
        "qkv_w": [dram("qkv_w0", w0.reshape(D, SLOTS, GROUPS, 3, HD).transpose(0, 3, 2, 1, 4).reshape(D, 3, D)),
                  dram("qkv_w1", w1.reshape(D, 3, SLOTS, GROUPS, HD).transpose(0, 1, 3, 2, 4).reshape(D, 3, D))],
        "qk_b": [dram(f"qk_b{k}", b[0:2].T) for k, b in enumerate(qkv_b)],
        "v_b": [dram("v_b0", b0.reshape(HEADS, 3, HD)[:, 2].reshape(D, 1)), dram("v_b1", b1[2 * D:].reshape(D, 1))],
        "out_w": [dram("out_w0", i["L0_attn_out_W"]), dram("out_w1", i["L1_attn_out_w"])],
        "out_b": [dram("out_b0", i["L0_attn_out_b"]), dram("out_b1", i["L1_attn_out_b"])],
        "gate": [dram("gate0", i["L0_ffn_gate"]), dram("gate1", i["L1_ffn_gate_kernel"])],
        "up": [[dram("up0", i["L0_ffn_W1"])], [dram("up1", i["L1_ffn_w0_kernel"]), dram("up2", i["L1_ffn_w1_kernel"])]],
        "down": [dram("down0", i["L0_ffn_W2"]), dram("down1", i["L1_ffn_wo_kernel"])],
        "b1": dram("b1", i["L0_ffn_b1"].reshape(EXPERTS, CHUNKS, P).transpose(2, 0, 1)),
        "b2": dram("b2", i["L0_ffn_b2"]),
    }
    x = dram("x", i["L0_attn_encodings"])
    out = nc.dram_tensor("out", x.shape, F32, kind="ExternalOutput").ap()
    build(nc, w, x, out)
    r = _run(nc, [arrays], core_ids=[0])
    return r.results[0]["out"]
```

```python
from contextlib import ExitStack

import concourse.bass as bass
from concourse import mybir

ALU = mybir.AluOpType
ACT = mybir.ActivationFunctionType
AX = mybir.AxisListType
F32 = mybir.dt.float32
F32R = mybir.dt.float32r
BF16 = mybir.dt.bfloat16

P = 128
D = 128
SEQ = 256
TILES = SEQ // P
HEADS = 16
HD = D // HEADS
GROUPS = 4
SLOTS = HEADS // GROUPS
EXPERTS = 8
HID = 256
CHUNKS = HID // P
EPS = 1e-5
SCALE = float(HD) ** -0.5
FILL = -10000.0
FLOOR = -FILL / SCALE
NEG = -1e30
RING = 3
VG, VC = 137, 32
VW = GROUPS * VG
HIDS = 4
ATTN_SLOTS, FFN_SLOTS = 12, 8
AHEAD = 7
UNITS = 3 * GROUPS


class Batch:

    def __init__(self, least, loop, count):
        self.exists = least >= 0 and least < count
        self.past = least >= count
        self.least = min(least, count - 1) if loop is None else least
        self.number = self.least if loop is None else loop * RING + least
        self.ring = self.least % RING
        self.turn = self.least // RING if loop is None else loop + least // RING


def pipeline(eng, count, deepest, slots, work, done=0, also=None):
    first = deepest
    while (count - first) % RING:
        first += 1
    for i in range(first):
        for slot in range(done if i == 0 else 0, slots):
            work(lambda back, i=i: Batch(i - back, None, count), slot)
    with eng.Fori(0, (count - first) // RING) as loop:
        for u in range(RING):
            for slot in range(slots):
                work(lambda back, u=u: Batch(first + u - back, loop, count), slot)
    for i in range(count, count + deepest):
        for slot in range(slots):
            work(lambda back, i=i: Batch(i - back, None, count), slot)
            if also:
                also(i, slot)


def run(eng, count, blocks):
    def start(back):
        return Batch(-back, None, count)

    for layer, (attention, prepare, feed_forward) in enumerate(blocks):
        def with_attention(i, slot):
            if i == count + 2 and slot < FFN_SLOTS:
                feed_forward(start, slot)
            if i == count + 3 and slot < FFN_SLOTS:
                prepare(slot)

        def with_feed_forward(i, slot):
            if i == count and slot < AHEAD:
                blocks[layer + 1][0](start, slot)
        pipeline(eng, count, 4, ATTN_SLOTS, attention, AHEAD if layer else 0, with_attention)
        pipeline(eng, count, 2, FFN_SLOTS, feed_forward, FFN_SLOTS, with_feed_forward if layer == 0 else None)


def build(nc, w, x_dram, out_dram):
    BATCHES = x_dram.shape[0]
    with ExitStack() as ctx:
        def sb(name, shape, dt=F32):
            return ctx.enter_context(nc.sbuf_tensor(name, shape, dt))

        def sem(name):
            return ctx.enter_context(nc.semaphore(name))

        X = sb("X", [P, BATCHES * TILES, D])
        kz = sb("kz", [P, RING, HEADS, SEQ], F32R)
        q_stack = sb("q_stack", [P, RING, GROUPS, SEQ], F32R)
        halves = sb("halves", [P, RING, 4, SEQ], F32R)
        probs = sb("probs", [P, GROUPS, SLOTS, 3 * P])
        v_pad = sb("v_pad", [P, RING, TILES, VW])
        xn = sb("xn", [P, TILES, D])
        xt_hi = sb("xt_hi", [P, RING, SEQ], F32R)
        xt_lo = sb("xt_lo", [P, RING, SEQ], F32R)
        stats = sb("stats", [P, TILES, 6])
        mv = sb("mv", [P, TILES, 2])
        rstd = sb("rstd", [P, TILES])
        var_eps = sb("var_eps", [P, TILES])
        minus_half = sb("minus_half", [P, TILES])
        x_shift = sb("x_shift", [P, TILES])
        neg_max = sb("neg_max", [P, RING, 3, HEADS])
        neg_m = sb("neg_m", [P, RING, TILES, HEADS])
        m_pad = sb("m_pad", [P, TILES, P], F32R)
        floor1 = sb("floor1", [P, 1])
        fill_bias = sb("fill_bias", [P, 1])
        c_fill = sb("c_fill", [P, RING, TILES, HEADS])
        c_u = sb("c_u", [P, RING, TILES * SLOTS, GROUPS, HD + 1])
        o_rows = sb("o_rows", [P, 2, SEQ])
        o_sum = sb("o_sum", [P, TILES * SLOTS, GROUPS, HD + 1])
        o_rden = sb("o_rden", [P, TILES * SLOTS * GROUPS])
        o_norm = sb("o_norm", [P, TILES, D])
        o_t = sb("o_t", [P, SEQ])
        ident = sb("ident", [P, P])
        mask = sb("mask", [P, P])
        later = sb("later", [P, 2, P])
        up_part = sb("up_part", [P, EXPERTS, HID], F32R)
        one_rows = sb("one_rows", [P, HEADS])
        raw_up = sb("raw_up", [P, EXPERTS, HID])
        w_raw = raw_up[:, :, :].rearrange("p e h -> p (e h)")[:, 0:2 * 3 * D].rearrange("p (l j d) -> p l j d", l=2, j=3)
        w_hi = sb("w_hi", [P, 2, 3, D], F32R)
        w_lo = sb("w_lo", [P, 2, 3, D], F32R)
        w_out = sb("w_out", [P, 2, D])
        b_qk = sb("b_qk", [P, 2, 2])
        b_v = sb("b_v", [P, 2])
        b_out = sb("b_out", [P, 2, D])
        gate_raw = sb("gate_raw", [P, 2, EXPERTS])
        gate_hi = sb("gate_hi", [P, 2, EXPERTS], F32R)
        gate_lo = sb("gate_lo", [P, 2, EXPERTS], F32R)
        w_down = sb("w_down", [P, EXPERTS, CHUNKS, D])
        b_up = sb("b_up", [P, EXPERTS, CHUNKS])
        b_down = sb("b_down", [P, D])
        rank = sb("rank", [P, TILES, EXPERTS])
        base_e = sb("base_e", [P, TILES, EXPERTS])
        gt = {k: sb(f"g_{k}", [P, TILES, EXPERTS]) for k in
              ("t", "e", "hot", "key", "sel1", "t2", "hot2", "key2", "sel2", "both", "we")}
        gs = {k: sb(f"gs_{k}", [P, TILES]) for k in ("v1", "mk1", "v2", "mk2", "sum", "rsum")}
        g_pad = sb("g_pad", [P, RING, TILES, P])
        g_rows = o_t
        raw_up2 = sb("raw_up2", [P, EXPERTS // 2, HID])
        q_flat = q_stack[:, :, :, :].rearrange("p a b c -> p (a b c)")
        k_flat = halves[:, :, :, :].rearrange("p a b c -> p (a b c)")
        s_flat = up_part[:, :, :].rearrange("p e h -> p (e h)")
        p_flat = probs[:, :, :, :].rearrange("p a b c -> p (a b c)")

        def up_w(k, part, e):
            if k and part:
                flat, at = (q_flat, k_flat)[e // 4], EXPERTS + e % 4
            else:
                flat, at = (k_flat if k else (q_flat, s_flat)[part]), e
            return flat[:, at * HID:(at + 1) * HID]

        def up_raw(k, e):
            return raw_up[:, e, :] if k == 0 else (raw_up2[:, e, :] if e < EXPERTS // 2 else rest2[:, e - EXPERTS // 2, :])
        rest2 = p_flat[:, 0:EXPERTS // 2 * HID].rearrange("p (e h) -> p e h", h=HID)
        hid = p_flat[:, EXPERTS * HID:(EXPERTS + HIDS * CHUNKS) * HID].rearrange("p (a c t) -> p a c t", a=HIDS, c=CHUNKS)
        silu = p_flat[:, (EXPERTS + HIDS * CHUNKS) * HID:(EXPERTS + HIDS * CHUNKS + 2 * CHUNKS) * HID].rearrange("p (a c t) -> p a c t", a=2, c=CHUNKS)

        ps = ctx.enter_context(nc.psum_tensor("ps", [P, 8, 512], F32))
        BS, BT, BO, BA, BR = (0, 1, 6), (2, 3), 4, 5, 7
        U0, U1, BYS, BTR, BG = (2, 3), (4, 7), ((1, 4), (1, 5)), 6, 0

        names = """ln_mv rstd_ok xn_ok t_ps xt_hi_ok xt_lo_ok qk_ps qk_hi_ok qk_lo_ok q_zero
            v_ps v_ok s_ps s_max m_ok mt_ps m_rep st_ps p_exp p_sel pv_ok o_rows_ok ot_ps o_norm_ok
            t2_ps o_t_ok y_ps x_ok u_ps c_ok cu_ok os_ok b_ok st_ok ag_ok nm_ok mh_ok rd_ok""".split()
        S = {n: sem("a_" + n) for n in names + ["r_ok"]}
        fnames = """ln_mv rstd_ok xn_ok t_ps xt_hi_ok xt_lo_ok lg_ps t_ok e_ok g_ok gt_ps gr_ok y9_ps y9_ok
            up_ps silu_ok hid_ok y_ps x_ok st_ok ag_ok top""".split()
        F = {n: sem("f_" + n) for n in fnames}
        stacks_in = [sem(f"stacks_in{r}") for r in range(RING)]
        x_first, x_rest = sem("x_first"), sem("x_rest")
        w_attn = [sem("w_attn0"), sem("w_attn1")]
        w_raw_in = [sem("w_raw_in0"), sem("w_raw_in1")]
        w_gate_in, w_ffn_in, w_split = sem("w_gate_in"), sem("w_ffn_in"), sem("w_split")
        up_in, up2_in, rest2_in, up_hi, up_split = sem("up_in"), sem("up2_in"), sem("rest2_in"), sem("up_hi"), sem("up_split")
        masks_ok, consts_dve, kz_ok = sem("masks_ok"), sem("consts_dve"), sem("kz_ok")
        kz_zero = sem("kz_zero")
        b_v_wide, b_v_ps, b_out_ok = sem("b_v_wide"), sem("b_v_ps"), sem("b_out_ok")
        dve_chain, pool_chain = sem("dve_chain"), sem("pool_chain")
        pool_passed, dve_passed = sem("pool_passed"), sem("dve_passed")
        stored = sem("stored")
        block = ctx.enter_context(nc.Block())

        def after(eng, s, b, per, count, base):
            if b.exists:
                eng.wait_ge(s, b.number * per + (base * per + count))
            elif b.past:
                eng.wait_ge(s, b.number * per + (base * per + per))

        STACK_DMAS = 3 * SLOTS + 3

        def stacks_done(eng, b, layer):
            if b.exists:
                eng.wait_ge(stacks_in[b.ring], (b.turn + (layer * TURNS[b.ring] + 1)) * (16 * STACK_DMAS))

        def tiles(b):
            return X[:, bass.ds(b.number * TILES, TILES), :]

        def one_tile(b, t):
            return X[:, b.number * TILES + t, :]

        def v_view(r, kt, n):
            return v_pad[:, r, kt, :].rearrange("p (g x) -> p g x", g=GROUPS)[:, :, 0:SLOTS * VC]\
                .rearrange("p g (c y) -> p g c y", c=SLOTS)[:, :, :, 0:n]

        TURNS = [(BATCHES - r + RING - 1) // RING for r in range(RING)]
        TOP = 15
        FIRST = 4
        x_view = x_dram.rearrange("b (t p) d -> p (b t) d", p=P)
        out_view = out_dram.rearrange("b (t p) d -> p (b t) d", p=P)

        @block.sync
        def _(sp):
            sp.dma_start(X[:, 0:FIRST * TILES, :], x_view[:, 0:FIRST * TILES, :]).then_inc(x_first, 16)
            for layer in range(2):
                sp.dma_start(w_raw[:, layer, :, :], w["qkv_w"][layer]).then_inc(w_raw_in[layer], 16)
                sp.dma_start(b_qk[:, layer, :], w["qk_b"][layer]).then_inc(w_attn[layer], 16)
                sp.dma_start(b_v[:, layer:layer + 1], w["v_b"][layer]).then_inc(w_attn[layer], 16)
                sp.dma_start(w_out[:, layer, :], w["out_w"][layer]).then_inc(w_attn[layer], 16)
                sp.dma_start(b_out[:, layer, :], w["out_b"][layer].partition_broadcast(P)).then_inc(w_attn[layer], 16)
            sp.dma_start(X[:, FIRST * TILES:, :], x_view[:, FIRST * TILES:, :]).then_inc(x_rest, 16)
            for layer in range(2):
                sp.dma_start(gate_raw[:, layer, :], w["gate"][layer]).then_inc(w_gate_in, 16)
            sp.dma_start(b_up[:, :, :], w["b1"]).then_inc(w_gate_in, 16)
            sp.wait_ge(consts_dve, 1)
            sp.dma_start(b_down[0:EXPERTS, :], w["b2"]).then_inc(w_gate_in, 16)

            def load_up(dst, up, signal):
                sp.dma_start(dst[:, :, :], up.rearrange("e d h -> d e h")).then_inc(signal, 16)

            def load_down(layer):
                sp.dma_start(w_down[:, :, :, :], w["down"][layer].rearrange("e (c p) d -> p e c d", p=P)).then_inc(w_ffn_in, 16)
            sp.wait_ge(w_split, 2)
            load_up(raw_up, w["up"][0][0], up_in)
            load_down(0)
            load_up(raw_up2, w["up"][1][1][0:EXPERTS // 2], up2_in)

            def sp_queries(b, part):
                sp.dma_start(q_stack[32 * part:32 * part + 32, b.ring, :, :].bitcast(F32), halves[:, b.ring, 2 * (part == 1), :].bitcast(F32))\
                  .then_inc(stacks_in[b.ring], 16)

            for layer in range(2):
                base = layer * BATCHES

                def step(at, slot):
                    b = at(0)
                    if b.exists:
                        after(sp, S["qk_hi_ok"], b, 1, 1, base)
                        after(sp, S["st_ps"], at(RING), UNITS, UNITS, base)
                        if b.least == 0:
                            sp.wait_ge(kz_zero, 1)
                        for part in (0, 1, 2):
                            if part == 2:
                                after(sp, S["q_zero"], b, 1, 1, base)
                                sp_queries(b, 0)
                                sp_queries(b, 2)
                                after(sp, S["qk_lo_ok"], b, 1, 1, base)
                                sp_queries(b, 1)
                            for c in range(SLOTS):
                                row = 32 * part + HD * c
                                dst = kz[row:row + HD, b.ring, :, :].rearrange("p (g c) t -> p g c t", c=SLOTS)[:, :, c, :]
                                sp.dma_start(dst.bitcast(F32), halves[32 * c:32 * c + 32, b.ring, 1 + 2 * (part == 2), :].bitcast(F32))\
                                  .then_inc(stacks_in[b.ring], 16)
                pipeline(sp, BATCHES, 4, 1, step)

                if layer == 0:
                    sp.wait_ge(up_split, EXPERTS)
                    load_up(raw_up, w["up"][1][0], up_in)
                    sp.wait_ge(F["x_ok"], BATCHES * EXPERTS)
                    load_down(1)
                else:
                    sp.wait_ge(S["pv_ok"], BATCHES * GROUPS * 2)
                    load_up(rest2, w["up"][1][1][EXPERTS // 2:], rest2_in)
            for b in range(0, BATCHES, 4):
                sp.wait_ge(F["x_ok"], EXPERTS * (BATCHES + b + 4))
                sp.dma_start(out_view[:, b * TILES:(b + 4) * TILES, :], X[:, b * TILES:(b + 4) * TILES, :]).then_inc(stored, 16)
            sp.wait_ge(stored, 16 * (BATCHES // 4))

        @block.gpsimd
        def _(pool):
            done = [0]

            def link(ins):
                done[0] += 1
                ins.then_inc(pool_chain, 1)
                pool.wait_ge(pool_chain, done[0])

            nc.gpsimd.memset(minus_half[:, :], -0.5)
            link(nc.gpsimd.memset(ident[:, :], 0.0))
            nc.gpsimd.affine_select(out=ident[:, :], in_=ident[:, :], compare_op=ALU.not_equal, fill=1.0,
                                    base=0, pattern=[[-1, P]], channel_multiplier=1).then_inc(masks_ok, 1)
            link(nc.gpsimd.memset(one_rows[:, :], 1.0))
            link(nc.gpsimd.affine_select(out=one_rows[:, :], in_=one_rows[:, :], compare_op=ALU.is_ge, fill=0.0,
                                         base=-96, pattern=[[-2, HEADS]], channel_multiplier=1))
            nc.gpsimd.affine_select(out=one_rows[:, :], in_=one_rows[:, :], compare_op=ALU.is_ge, fill=0.0,
                                    base=97, pattern=[[2, HEADS]], channel_multiplier=-1).then_inc(masks_ok, 1)
            link(nc.gpsimd.memset(mask[:, :], 0.0))
            nc.gpsimd.affine_select(out=mask[:, :], in_=mask[:, :], compare_op=ALU.is_ge, fill=NEG,
                                    base=0, pattern=[[-1, P]], channel_multiplier=1).then_inc(masks_ok, 1)
            link(nc.gpsimd.memset(later[:, :, :], 1.0))
            nc.gpsimd.affine_select(out=later[:, 0, :], in_=later[:, 0, :], compare_op=ALU.is_gt, fill=0.0,
                                    base=0, pattern=[[-1, P]], channel_multiplier=1).then_inc(masks_ok, 1)
            link(nc.gpsimd.memset(floor1[:, :], FLOOR))
            nc.gpsimd.affine_select(out=floor1[:, :], in_=floor1[:, :], compare_op=ALU.not_equal, fill=3e38,
                                    base=-(P - 1), pattern=[[0, 1]], channel_multiplier=1).then_inc(masks_ok, 1)
            for r in range(RING):
                ins = nc.gpsimd.memset(kz[0:96, r, :, :].bitcast(F32), 0.0)
            ins.then_inc(kz_zero, 1)
            def parts(layer):
                base = layer * BATCHES

                def rstd_of(b, M):
                    after(pool, M["ln_mv"], b, 1, 1, base)
                    ins = nc.gpsimd.tensor_tensor(rstd[:, :], var_eps[:, :], minus_half[:, :], ALU.pow)
                    if M is F:
                        ins.then_inc(F["rstd_ok"], 1)
                    else:
                        ins.then_inc(S["r_ok"], 1)
                        after(pool, S["r_ok"], b, 1, 1, base)
                        pool.sem_inc(pool_passed)
                        for t in range(TILES):
                            ins = nc.gpsimd.tensor_scalar(x_shift[:, t:t + 1], mv[:, t, 0:1], -1.0, rstd[:, t:t + 1], ALU.mult, ALU.mult)
                        ins.then_inc(S["rstd_ok"], 1)

                def select_unit(b, g, kind):
                    after(pool, S["p_exp"], b, UNITS, 3 * g + kind + 1, base)
                    pool.sem_inc(pool_passed)
                    view = probs[:, g, :, (kind - 1) * SEQ:(kind - 1) * SEQ + P]
                    nc.gpsimd.affine_select(out=view, in_=view, compare_op=ALU.is_ge, fill=0.0, base=0,
                                            pattern=[[0, SLOTS], [1, P]], channel_multiplier=-1).then_inc(S["p_sel"], 1)

                def attention(at, slot):
                    b0, b2, b3, b4 = at(0), at(2), at(3), at(4)
                    if slot == 0 and b0.exists:
                        rstd_of(b0, S)
                    if slot == 2 and b0.exists:
                        after(pool, S["xn_ok"], b0, 1, 1, base)
                        if b0.least == 0 and layer == 0:
                            pool.wait_ge(b_out_ok, 2)
                        nc.gpsimd.tensor_tensor(tiles(b0), tiles(b0), b_out[:, layer, :].unsqueeze(1).broadcast_to([P, TILES, D]),
                                                ALU.add).then_inc(S["b_ok"], 1)
                    if slot == 7 and b0.exists:
                        if layer and b0.least == 0:
                            pool.wait_ge(F["y_ps"], BATCHES * EXPERTS)
                        after(pool, S["st_ps"], at(RING), UNITS, UNITS, base)
                        pool.sem_inc(pool_passed)
                        nc.gpsimd.memset(q_stack[:, b0.ring, :, :].bitcast(F32), 0.0).then_inc(S["q_zero"], 1)
                    if slot == 2 and b4.exists and layer == 0:
                        after(pool, S["rd_ok"], b4, 1, 1, base)
                        nc.gpsimd.tensor_tensor(o_norm[:, :, :].rearrange("p t (h r) -> p (t h) r", r=HD), o_sum[:, :, :, :].rearrange("p a g r -> p (a g) r")[:, :, 0:HD],
                                                o_rden[:, :].unsqueeze(2).broadcast_to([P, TILES * HEADS, HD]), ALU.mult).then_inc(S["o_norm_ok"], 1)
                    b, u = (b2, slot - 9) if slot >= 9 else (b3, slot + 3)
                    if b.exists and u % 3:
                        select_unit(b, u // 3, u % 3)

                def feed_forward(at, slot):
                    b0 = at(0)
                    if slot == 0 and b0.exists:
                        rstd_of(b0, F)
                    if slot == 6 and b0.exists:
                        after(pool, F["t_ok"], b0, 1, 1, base)
                        nc.gpsimd.tensor_tensor(gt["e"][:, :, :], base_e[:, :, :], gt["t"][:, :, :], ALU.pow).then_inc(F["e_ok"], 1)
                return attention, lambda slot: None, feed_forward

            run(pool, BATCHES, [parts(0), parts(1)])

        @block.scalar
        def _(act):
            act.wait_ge(consts_dve, 1)
            act.wait_ge(masks_ok, 2)
            for r in range(RING - 1):
                ins = nc.scalar.activation(kz[96:P, r, :, :], one_rows[96:P, :].unsqueeze(2).broadcast_to([32, HEADS, SEQ]), ACT.Copy)
            ins.then_inc(kz_ok, 1)

            def norm_t_hi(b, M, base):
                after(act, M["t_ps"], b, 1, 1, base)
                nc.scalar.activation(xt_hi[:, b.ring, :], ps[:, BA if M is S else BTR, 0:SEQ], ACT.Copy).then_inc(M["xt_hi_ok"], 1)

            def parts(layer):
                base = layer * BATCHES

                def attention(at, slot):
                    b0, b1, b2, b3, b4 = (at(i) for i in range(5))
                    b, u = (b2, slot - 9) if slot >= 9 else (b3, slot + 3)
                    if b.exists:
                        g, kind = u // 3, u % 3
                        after(act, S["st_ps"], b, UNITS, u + 1, base)
                        p = at(3) if slot >= 9 else at(4)
                        if kind == 0:
                            after(act, S["pv_ok"], p, GROUPS, g + 1, base)
                        dst = (probs[:, g, 0:2, 0:SEQ], probs[:, g, 2:4, 0:SEQ], probs[:, g, :, SEQ:3 * P])[kind]
                        nc.scalar.activation(dst, ps[:, BT[u % 2], :].rearrange("p (c q) -> p c q", q=SEQ if kind < 2 else P), ACT.Exp, scale=SCALE)\
                          .then_inc(S["p_exp"], 1)
                    if slot == 1 and b0.exists:
                        after(act, S["rstd_ok"], b0, 1, 1, base)
                        after(act, S["t_ps"], b1, 1, 1, base)
                        for t in range(TILES):
                            ins = nc.scalar.activation(xn[:, t, :], X[:, b0.number * TILES + t, :], ACT.Identity, bias=x_shift[:, t:t + 1], scale=rstd[:, t:t + 1])
                        ins.then_inc(S["xn_ok"], 1)
                    if slot == 0 and b4.exists:
                        after(act, S["pv_ok"], b4, GROUPS, GROUPS, base)
                        after(act, S["ot_ps"], at(5), 1, 1, base)
                        nc.scalar.activation(o_rows[:, :, :].rearrange("p a t -> p (a t)"), ps[:, BO, :], ACT.Copy)\
                          .then_inc(S["o_rows_ok"], 1)
                    if slot == 1 and b1.exists:
                        after(act, S["v_ps"], b1, 1, 1, base)
                        after(act, S["pv_ok"], b4, GROUPS, GROUPS, base)
                        for t in range(TILES):
                            ins = nc.scalar.activation(v_view(b1.ring, t, HD), ps[:, BA, t * P:(t + 1) * P].rearrange("p (g c r) -> p g c r", g=GROUPS, c=SLOTS), ACT.Copy)
                        ins.then_inc(S["v_ok"], 1)
                    if slot == 5 and b4.exists:
                        after(act, S["t2_ps"], b4, 1, 1, base)
                        nc.scalar.activation(o_t[:, :], ps[:, BR, 0:SEQ], ACT.Copy).then_inc(S["o_t_ok"], 1)
                    if slot == 3 and b0.exists:
                        norm_t_hi(b0, S, base)
                    if slot == 5 and b0.exists:
                        if b0.least == 0:
                            act.wait_ge(w_attn[layer], 64)
                        after(act, S["qk_ps"], b0, 1, 1, base)
                        stacks_done(act, at(RING), layer)
                        for t in range(2):
                            ins = nc.scalar.activation(halves[:, b0.ring, t, :], ps[:, BA, t * SEQ:(t + 1) * SEQ], ACT.Identity, bias=b_qk[:, layer, t:t + 1])
                        ins.then_inc(S["qk_hi_ok"], 1)
                    if slot == 7 and b2.exists:
                        after(act, S["mt_ps"], b2, 1, 1, base)
                        after(act, S["s_ps"], b2, UNITS, UNITS, base)
                        nc.scalar.activation(q_stack[96:P, b2.ring, :, :], ps[96:P, BA, 0:SEQ].unsqueeze(1).broadcast_to([32, GROUPS, SEQ]), ACT.Copy)\
                          .then_inc(S["m_rep"], 1)
                        if layer == 0:
                            after(act, S["cu_ok"], at(2 + RING), 1, 1, base)
                            nc.scalar.activation(c_fill[:, b2.ring, :, :], neg_m[:, b2.ring, :, :], ACT.Exp, bias=fill_bias[:, :], scale=SCALE)\
                              .then_inc(S["c_ok"], 1)

                def feed_forward(at, slot):
                    b0, b1, b2 = at(0), at(1), at(2)
                    if slot == 2 and b0.exists:
                        norm_t_hi(b0, F, base)
                    if slot == 3 and b1.exists and layer == 0:
                        after(act, F["gt_ps"], b1, 1, 1, base)
                        after(act, F["y9_ps"], b2, 1, 1, base)
                        nc.scalar.activation(g_rows[:, :], ps[:, BG, 0:SEQ], ACT.Copy).then_inc(F["gr_ok"], 1)
                    if b1.exists:
                        e = slot
                        after(act, F["up_ps"], b1, EXPERTS, e + 1, base)
                        if layer == 0:
                            if b1.least == 0 and e == 0:
                                act.wait_ge(w_gate_in, 64)
                            if e >= HIDS:
                                after(act, F["y_ps"], b1, EXPERTS, e - HIDS + 1, base)
                            else:
                                after(act, F["y_ps"], b2, EXPERTS, EXPERTS - HIDS + 1 + e, base)
                            for ch in range(CHUNKS):
                                ins = nc.scalar.activation(hid[:, e % HIDS, ch, :], ps[:, U0[e % 2], ch * SEQ:(ch + 1) * SEQ], ACT.Relu, bias=b_up[:, e, ch:ch + 1])
                            ins.then_inc(F["hid_ok"], 1)
                        else:
                            if e >= 2:
                                after(act, F["hid_ok"], b1, EXPERTS, e - 1, base)
                            else:
                                after(act, F["hid_ok"], at(2), EXPERTS, EXPERTS - 1 + e, base)
                            nc.scalar.activation(silu[:, e % 2, :, :].rearrange("p c t -> p (c t)"), ps[:, U0[e % 2], :], ACT.Silu).then_inc(F["silu_ok"], 1)
                def prepare(e):
                    if e == 0:
                        act.wait_ge(S["pv_ok"], BATCHES * GROUPS * (layer + 1))
                        for r in range(RING):
                            act.wait_ge(stacks_in[r], 16 * STACK_DMAS * TURNS[r] * (layer + 1))
                        act.wait_ge(up_in, 16 * (layer + 1))
                        if layer:
                            act.wait_ge(up2_in, 16)
                    if e == EXPERTS // 2 and layer:
                        act.wait_ge(rest2_in, 16)
                    for k in range(1 + layer):
                        nc.scalar.activation(up_w(k, 0, e), up_raw(k, e), ACT.Copy).then_inc(up_hi, 1)
                return attention, prepare, feed_forward

            run(act, BATCHES, [parts(0), parts(1)])

        @block.tensor
        def _(pe):
            for layer in range(2):
                pe.wait_ge(w_attn[layer], 64)
                pe.wait_ge(b_v_wide, layer + 1)
                pe.wait_ge(consts_dve, 1)
                nc.tensor.matmul(ps[:, BR, layer * D:(layer + 1) * D], o_norm[:, layer, :], w_out[:, layer, :], start=True, stop=True, skip_group_check=True).then_inc(b_v_ps, 1)
            def parts(layer):
                base = layer * BATCHES
                def turn_norm(b, M, bank):
                    after(pe, M["xn_ok"], b, 1, 1, base)
                    if b.least == 0 and M is S and layer == 0:
                        pe.wait_ge(masks_ok, 1)
                    for t in range(TILES):
                        ins = nc.tensor.transpose(ps[:, bank, t * P:(t + 1) * P], xn[:, t, :], ident[:, :])
                    ins.then_inc(M["t_ps"], 1)

                def attention(at, slot):
                    b0, b1, b2, b3, b4 = (at(i) for i in range(5))
                    b, u = (b1, slot - 6) if slot >= 6 else (b2, slot + 6)
                    if b.exists:
                        g, kind = u // 3, u % 3
                        qt, kt = (0, 1, 1)[kind], (0, 0, 1)[kind]
                        if u == 0:
                            if b.least == 0 and layer == 0:
                                pe.wait_ge(kz_ok, 2)
                            stacks_done(pe, b, layer)
                        if u >= 3:
                            after(pe, S["s_max"], b, UNITS, u - 2, base)
                        else:
                            after(pe, S["s_max"], at(2), UNITS, UNITS - 2 + u, base)
                        bank = ps[:, BS[u % 3], :]
                        nc.tensor.matmul(bank, q_stack[:, b.ring, g, qt * P:(qt + 1) * P], kz[:, b.ring, g * SLOTS:(g + 1) * SLOTS, kt * P:(kt + 1) * P],
                                         start=True, stop=True, skip_group_check=True).then_inc(S["s_ps"], 1)
                    if slot == 8 and b2.exists:
                        after(pe, S["m_ok"], b2, 1, 1, base)
                        after(pe, S["qk_lo_ok"], b0, 1, 1, base)
                        after(pe, S["xt_lo_ok"], b0, 1, 1, base)
                        for t in range(TILES):
                            ins = nc.tensor.transpose(ps[:, BA, t * P:(t + 1) * P], m_pad[:, t, :].bitcast(F32), ident[:, :])
                        ins.then_inc(S["mt_ps"], 1)
                    b, u = (b2, slot - 9) if slot >= 9 else (b3, slot + 3)
                    if b.exists:
                        g, kind = u // 3, u % 3
                        if u == 0:
                            after(pe, S["m_rep"], b, 1, 1, base)
                        if u >= 2:
                            after(pe, S["p_exp"], b, UNITS, u - 1, base)
                        else:
                            after(pe, S["p_exp"], at(3), UNITS, UNITS - 1 + u, base)
                        heads, kt = (range(2), range(2, 4), range(4))[kind], kind // 2
                        for j, c in enumerate(heads):
                            n = SEQ - kt * P
                            ins = nc.tensor.matmul(ps[:, BT[u % 2], j * n:(j + 1) * n], kz[:, b.ring, g * SLOTS + c, kt * P:(kt + 1) * P],
                                                   q_stack[:, b.ring, g, kt * P:], start=True, stop=True, skip_group_check=True)
                        ins.then_inc(S["st_ps"], 1)
                    if slot in (2, 5, 8, 11) and b3.exists:
                        g = (slot - 2) // 3
                        after(pe, S["p_sel"], b3, 2 * GROUPS, 2 * g + 2, base)
                        if g == 0:
                            after(pe, S["v_ok"], b3, 1, 1, base)
                            after(pe, S["o_rows_ok"], b4, 1, 1, base)
                        col = 0 if g < 3 else SEQ
                        for kt in range(TILES):
                            for c in range(SLOTS):
                                lo = g * P + c * VC if g < 3 else 3 * VG + c * VC
                                ins = nc.tensor.matmul(ps[32 * c:32 * c + 32, BO, col + kt * P:col + SEQ], v_pad[:, b3.ring, kt, lo:lo + 32],
                                                       probs[:, g, c, 0:SEQ] if kt == 0 else probs[:, g, c, SEQ:3 * P],
                                                       start=(kt == 0 and g in (0, 3)), stop=(kt == 1), skip_group_check=True)
                        ins.then_inc(S["pv_ok"], 1)
                    if slot == 2 and b4.exists:
                        after(pe, S["o_rows_ok"], b4, 1, 1, base)
                        after(pe, S["x_ok"], at(5), 1, 1, base)
                        for half in range(2):
                            for t in range(TILES):
                                ins = nc.tensor.transpose(ps[:, BR, (2 * half + t) * P:(2 * half + t + 1) * P], o_rows[:, half, t * P:(t + 1) * P], ident[:, :])
                        ins.then_inc(S["ot_ps"], 1)
                    if slot == 5 and b4.exists:
                        after(pe, S["o_norm_ok"], b4, 1, 1, base)
                        for t in range(TILES):
                            ins = nc.tensor.transpose(ps[:, BR, t * P:(t + 1) * P], o_norm[:, t, :], ident[:, :])
                        ins.then_inc(S["t2_ps"], 1)
                    if slot == 6 and b4.exists:
                        after(pe, S["o_t_ok"], b4, 1, 1, base)
                        for t in range(TILES):
                            ins = nc.tensor.matmul(ps[:, BR, SEQ + t * P:SEQ + (t + 1) * P], o_t[:, t * P:(t + 1) * P], w_out[:, layer, :], start=True, stop=True, skip_group_check=True)
                        ins.then_inc(S["y_ps"], 1)
                    if slot == 2 and b1.exists:
                        after(pe, S["m_rep"], b3, 1, 1, base)
                        after(pe, S["qk_lo_ok"], b1, 1, 1, base)
                        if layer == 0:
                            after(pe, S["cu_ok"], b3, 1, 1, base)
                        after(pe, S["xt_lo_ok"], b1, 1, 1, base)
                        for t in range(TILES):
                            for j, (a, ww) in enumerate(((xt_hi, w_hi), (xt_lo, w_hi), (xt_hi, w_lo))):
                                ins = nc.tensor.matmul(ps[:, BA, t * P:(t + 1) * P], a[:, b1.ring, t * P:(t + 1) * P], ww[:, layer, 2, :], start=(j == 0), stop=(j == 2), skip_group_check=True)
                        ins.then_inc(S["v_ps"], 1)
                    if slot == 3 and b0.exists:
                        after(pe, S["v_ok"], b1, 1, 1, base)
                        turn_norm(b0, S, BA)
                    if slot == 5 and b0.exists:
                        after(pe, S["xt_lo_ok"], b0, 1, 1, base)
                        if b0.least == 0:
                            pe.wait_ge(w_split, 2)
                        after(pe, S["qk_lo_ok"], b1, 1, 1, base)
                        if layer == 0:
                            after(pe, S["cu_ok"], b3, 1, 1, base)
                        for t in range(2):
                            for j, (a, ww) in enumerate(((xt_hi, w_hi), (xt_lo, w_hi), (xt_hi, w_lo))):
                                ins = nc.tensor.matmul(ps[:, BA, t * SEQ:(t + 1) * SEQ], ww[:, layer, t, :], a[:, b0.ring, :], start=(j == 0), stop=(j == 2), skip_group_check=True)
                        ins.then_inc(S["qk_ps"], 1)
                    if slot == 0 and b3.exists and layer == 0:
                        if b3.least == 0:
                            pe.wait_ge(masks_ok, 5)
                        after(pe, S["v_ok"], b3, 1, 1, base)
                        after(pe, S["qk_lo_ok"], b1, 1, 1, base)
                        after(pe, S["m_rep"], b3, 1, 1, base)
                        for t, kt, m, first in ((0, 0, 0, True), (0, 1, 1, False), (1, 1, 0, True)):
                            vv = v_view(b3.ring, kt, HD + 1)
                            ins = nc.tensor.matmul(ps[:, BA, t * 144:(t + 1) * 144], later[:, m, :], vv, start=first, stop=(kt == 1), skip_group_check=True)
                        ins.then_inc(S["u_ps"], 1)

                ups = 1 if layer == 0 else 2

                def feed_forward(at, slot):
                    b0, b1, b2 = at(0), at(1), at(2)
                    if slot == 3 and b1.exists and layer == 0:
                        after(pe, F["g_ok"], b1, 1, 1, base)
                        for t in range(TILES):
                            ins = nc.tensor.transpose(ps[:, BG, t * P:(t + 1) * P], g_pad[:, b1.ring, t, :], ident[:, :])
                        ins.then_inc(F["gt_ps"], 1)
                    if slot == 4 and b1.exists and layer == 0:
                        after(pe, F["gr_ok"], b1, 1, 1, base)
                        after(pe, F["y9_ok"], b2, 1, 1, base)
                        for t in range(TILES):
                            ins = nc.tensor.matmul(ps[:, BG, SEQ + t * P:SEQ + (t + 1) * P], g_rows[:, t * P:(t + 1) * P], b_down[:, :], start=True, stop=True, skip_group_check=True)
                        ins.then_inc(F["y9_ps"], 1)
                    if b1.exists:
                        e = slot
                        if e == 0:
                            after(pe, F["xt_lo_ok"], b1, 1, 1, base)
                        if b1.least == 0:
                            if e == 0:
                                pe.wait_ge(S["x_ok"], BATCHES * (layer + 1))
                                pe.wait_ge(w_ffn_in, 16 * (layer + 1))
                            pe.wait_ge(up_split, EXPERTS * layer + ups * (e + 1))
                        free = F["hid_ok"]
                        if e >= 2:
                            after(pe, free, b1, EXPERTS, e - 1, base)
                        else:
                            after(pe, free, at(2), EXPERTS, EXPERTS - 1 + e, base)
                        for k in range(ups):
                            bank = (U0, U1)[k][e % 2]
                            for ch in range(CHUNKS):
                                for j, (a, part) in enumerate(((xt_hi, 0), (xt_lo, 0), (xt_hi, 1))):
                                    ins = nc.tensor.matmul(ps[:, bank, ch * SEQ:(ch + 1) * SEQ], up_w(k, part, e)[:, ch * P:(ch + 1) * P], a[:, b1.ring, :], start=(j == 0), stop=(j == 2), skip_group_check=True)
                        ins.then_inc(F["up_ps"], 1)
                    b, e = (b1, slot - 2) if slot >= 2 else (b2, slot + EXPERTS - 2)
                    if b.exists:
                        after(pe, F["hid_ok"], b, EXPERTS, e + 1, base)
                        if e >= 2:
                            after(pe, F["x_ok"], b, EXPERTS, e - 1, base)
                        else:
                            after(pe, F["x_ok"], b2, EXPERTS, EXPERTS - 1 + e, base)
                        for t in range(TILES):
                            for ch in range(CHUNKS):
                                ins = nc.tensor.matmul(ps[:, BYS[layer][e % 2], t * P:(t + 1) * P], hid[:, e % HIDS, ch, t * P:(t + 1) * P], w_down[:, e, ch, :], start=(ch == 0), stop=(ch == 1), skip_group_check=True)
                        ins.then_inc(F["y_ps"], 1)
                    if slot == 2 and b0.exists:
                        after(pe, F["xt_lo_ok"], b1, 1, 1, base)
                        turn_norm(b0, F, BTR)
                    if slot == 4 and b0.exists:
                        if b0.least == 0:
                            pe.wait_ge(w_gate_in, 64)
                            pe.wait_ge(w_split, 3)
                        after(pe, F["xt_lo_ok"], b0, 1, 1, base)
                        if layer == 0:
                            after(pe, F["gr_ok"], b1, 1, 1, base)
                        else:
                            after(pe, F["t_ok"], b1, 1, 1, base)
                        for t in range(TILES):
                            for j, (a, ww) in enumerate(((xt_hi, gate_hi), (xt_lo, gate_hi), (xt_hi, gate_lo))):
                                ins = nc.tensor.matmul(ps[:, BG, t * EXPERTS:(t + 1) * EXPERTS], a[:, b0.ring, t * P:(t + 1) * P], ww[:, layer, :], start=(j == 0), stop=(j == 2), skip_group_check=True)
                        ins.then_inc(F["lg_ps"], 1)
                return attention, lambda slot: None, feed_forward

            run(pe, BATCHES, [parts(0), parts(1)])

        @block.vector
        def _(dve):
            for r in range(RING):
                nc.vector.memset(v_pad[:, r, :, :], 0.0)
                nc.vector.memset(g_pad[:, r, :, :], 0.0)
            nc.vector.memset(m_pad[:, :, :].bitcast(F32), 0.0)
            nc.vector.memset(fill_bias[:, :], FILL)
            nc.vector.memset(base_e[:, :, :], 2.718281828459045)
            for e in range(EXPERTS):
                nc.vector.memset(rank[:, :, e], float(EXPERTS - e))
            nc.vector.memset(b_down[:, :], 0.0).then_inc(dve_chain, 1)
            dve.wait_ge(dve_chain, 1)
            for r in range(RING):
                for g in range(GROUPS):
                    at = g * VG + HD
                    ins = nc.vector.memset(v_pad[:, r, :, at:at + 3 * VC + 1:VC], 1.0)
            ins.then_inc(consts_dve, 1)
            chain = [1]

            def link(ins):
                chain[0] += 1
                ins.then_inc(dve_chain, 1)
                dve.wait_ge(dve_chain, chain[0])

            for layer in range(2):
                dve.wait_ge(w_attn[layer], 64)
                nc.vector.tensor_copy(o_norm[:, layer, :], b_v[:, layer:layer + 1].broadcast_to([P, D])).then_inc(b_v_wide, 1)
                dve.wait_ge(w_raw_in[layer], 16)
                link(nc.vector.tensor_copy(w_hi[:, layer, :, :], w_raw[:, layer, :, :]))
                nc.vector.tensor_tensor(w_lo[:, layer, :, :], w_raw[:, layer, :, :], w_hi[:, layer, :, :].bitcast(F32), ALU.subtract).then_inc(w_split, 1)
            dve.wait_ge(b_v_ps, 2)
            for layer in range(2):
                nc.vector.tensor_tensor(b_out[:, layer, :], b_out[:, layer, :], ps[:, BR, layer * D:(layer + 1) * D], ALU.add).then_inc(b_out_ok, 1)
            dve.wait_ge(masks_ok, 2)
            nc.vector.tensor_copy(kz[96:P, RING - 1, :, :], one_rows[96:P, :].unsqueeze(2).broadcast_to([32, HEADS, SEQ])).then_inc(kz_ok, 1)

            def parts(layer):
                base = layer * BATCHES

                def stats_of(b, M, fill=lambda pieces: None):
                    if M is F:
                        after(dve, S["x_ok"], b, 1, 1, base)
                    elif layer:
                        after(dve, F["x_ok"], b, EXPERTS, EXPERTS, 0)
                    for t in range(TILES):
                        ins = nc.vector.bn_stats(stats[:, t, :], one_tile(b, t))
                    ins.then_inc(M["st_ok"], 1)
                    fill(1)
                    after(dve, M["st_ok"], b, 1, 1, base)
                    dve.sem_inc(dve_passed)
                    for t in range(TILES):
                        ins = nc.vector.bn_aggr(mv[:, t, :], stats[:, t, :])
                    ins.then_inc(M["ag_ok"], 1)
                    fill(2)
                    after(dve, M["ag_ok"], b, 1, 1, base)
                    nc.vector.tensor_scalar(var_eps[:, :], mv[:, :, 1], EPS, None, ALU.add).then_inc(M["ln_mv"], 1)

                def norm_of(b):
                    after(dve, F["rstd_ok"], b, 1, 1, base)
                    for t in range(TILES):
                        ins = nc.vector.tensor_scalar(xn[:, t, :], one_tile(b, t), mv[:, t, 0:1], rstd[:, t:t + 1], ALU.subtract, ALU.mult)
                    ins.then_inc(F["xn_ok"], 1)

                def norm_t_lo(b, M):
                    after(dve, M["xt_hi_ok"], b, 1, 1, base)
                    nc.vector.tensor_tensor(xt_lo[:, b.ring, :], ps[:, BA if M is S else BTR, 0:SEQ], xt_hi[:, b.ring, :].bitcast(F32), ALU.subtract).then_inc(M["xt_lo_ok"], 1)

                def attention(at, slot):
                    b0, b1, b2, b3, b4 = (at(i) for i in range(5))
                    b, u = (b1, slot - 6) if slot >= 6 else (b2, slot + 6)
                    g, kind = u // 3, u % 3
                    sent = [0]

                    def maximum(pieces):
                        for c in range(sent[0], pieces if b.exists else 0):
                            if c == 0:
                                if u == 0 and b.least == 0 and layer == 0:
                                    dve.wait_ge(masks_ok, 5)
                                after(dve, S["s_ps"], b, UNITS, u + 1, base)
                            if kind != 1:
                                if c == 0:
                                    dve.sem_inc(dve_passed)
                                ins = nc.vector.tensor_tensor_reduce(out=ps[:, BS[u % 3], c * P:(c + 1) * P], in0=ps[:, BS[u % 3], c * P:(c + 1) * P], in1=mask[:, :], scale=-1.0, scalar=3e38,
                                                                     op0=ALU.add, op1=ALU.min, accum_out=neg_max[:, b.ring, kind, g * SLOTS + c:g * SLOTS + c + 1])
                            elif c == 0:
                                ins = nc.vector.tensor_reduce(neg_max[:, b.ring, kind, g * SLOTS:(g + 1) * SLOTS], ps[:, BS[u % 3], :].rearrange("p (c k) -> p c k", c=SLOTS),
                                                              AX.X, ALU.max, negate=True)
                            if c == (0 if kind == 1 else SLOTS - 1):
                                ins.then_inc(S["s_max"], 1)
                        sent[0] = max(sent[0], pieces)

                    if slot == 0 and b0.exists:
                        if layer == 0 and b0.least == 0:
                            dve.wait_ge(x_first, 16)
                        if layer == 0 and b0.least == FIRST:
                            dve.wait_ge(x_rest, 16)
                        stats_of(b0, S, maximum)
                    if slot == 1 and b3.exists and layer == 0:
                        after(dve, S["u_ps"], b3, 1, 1, base)
                        after(dve, S["c_ok"], b3, 1, 1, base)
                        for t in range(TILES):
                            out = c_u[:, b3.ring, t * SLOTS:(t + 1) * SLOTS, :, :]
                            ins = nc.vector.tensor_tensor(out, ps[:, BA, t * 144:(t + 1) * 144].rearrange("p (g c r) -> p c g r", g=GROUPS, c=SLOTS),
                                                          c_fill[:, b3.ring, t, :].rearrange("p (g c) -> p c g", g=GROUPS).unsqueeze(3).broadcast_to([P, SLOTS, GROUPS, HD + 1]), ALU.mult)
                        ins.then_inc(S["cu_ok"], 1)
                    if slot == 6 and b2.exists:
                        nm, m = neg_max[:, b2.ring, :, :], neg_m[:, b2.ring, :, :]
                        after(dve, S["s_max"], b2, UNITS, UNITS, base)
                        if layer == 0:
                            after(dve, S["c_ok"], at(2 + RING), 1, 1, base)
                            nc.vector.tensor_scalar(m[:, 0, :], nm[:, 0, :], FLOOR, None, ALU.min)
                            nc.vector.scalar_tensor_tensor(out=m[:, 1, :], in0=nm[:, 1, :], scalar=floor1[:, 0:1], in1=nm[:, 2, :], op0=ALU.min, op1=ALU.min).then_inc(S["nm_ok"], 1)
                        else:
                            nc.vector.tensor_copy(m[:, 0, :], nm[:, 0, :])
                            nc.vector.tensor_tensor(m[:, 1, :], nm[:, 1, :], nm[:, 2, :], ALU.min).then_inc(S["nm_ok"], 1)
                        maximum(1)
                        after(dve, S["nm_ok"], b2, 1, 1, base)
                        after(dve, S["mt_ps"], at(3), 1, 1, base)
                        nc.vector.tensor_copy(m_pad[:, :, 96:P:2], m).then_inc(S["mh_ok"], 1)
                        maximum(2)
                        after(dve, S["mh_ok"], b2, 1, 1, base)
                        nc.vector.tensor_tensor(m_pad[:, :, 97:P:2], m, m_pad[:, :, 96:P:2].bitcast(F32), ALU.subtract).then_inc(S["m_ok"], 1)
                    if slot == 6 and b0.exists:
                        after(dve, S["qk_hi_ok"], b0, 1, 1, base)
                        for t in range(2):
                            ins = nc.vector.scalar_tensor_tensor(out=halves[:, b0.ring, 2 + t, :], in0=ps[:, BA, t * SEQ:(t + 1) * SEQ], scalar=b_qk[:, layer, t:t + 1],
                                                                 in1=halves[:, b0.ring, t, :].bitcast(F32), op0=ALU.add, op1=ALU.subtract)
                        ins.then_inc(S["qk_lo_ok"], 1)
                    maximum(SLOTS)
                    if slot == 2 and b4.exists:
                        after(dve, S["ot_ps"], b4, 1, 1, base)
                        sums = [(gg, ps[:, BR, part * SEQ:(part + 1) * SEQ].rearrange("p (a b) -> p a b", b=32)[:, :, 0:(HD + 1) * n].rearrange("p a (g r) -> p a g r", g=n))
                                for part, gg, n in ((0, slice(0, 3), 3), (1, slice(3, 4), 1))]
                        rden = o_rden[:, :].rearrange("p (a g) -> p a g", g=GROUPS)
                        if layer == 0:
                            for gg, src in sums:
                                ins = nc.vector.tensor_tensor(o_sum[:, :, gg, :], src, c_u[:, b4.ring, :, gg, :], ALU.add)
                            ins.then_inc(S["os_ok"], 1)
                            after(dve, S["os_ok"], b4, 1, 1, base)
                            nc.vector.reciprocal(rden, o_sum[:, :, :, HD]).then_inc(S["rd_ok"], 1)
                        else:
                            for gg, src in sums:
                                ins = nc.vector.reciprocal(rden[:, :, gg], src[:, :, :, HD])
                            ins.then_inc(S["rd_ok"], 1)
                            after(dve, S["rd_ok"], b4, 1, 1, base)
                            for gg, src in sums:
                                ins = nc.vector.tensor_tensor(o_norm[:, :, :].rearrange("p t (c g r) -> p (t c) g r", g=GROUPS, r=HD)[:, :, gg, :], src[:, :, :, 0:HD],
                                                              rden[:, :, gg].unsqueeze(3).broadcast_to([P, TILES * SLOTS, gg.stop - gg.start, HD]), ALU.mult)
                            ins.then_inc(S["o_norm_ok"], 1)
                    if slot == 3 and b0.exists:
                        norm_t_lo(b0, S)
                    if slot == 8 and b4.exists:
                        after(dve, S["y_ps"], b4, 1, 1, base)
                        after(dve, S["b_ok"], b4, 1, 1, base)
                        nc.vector.tensor_tensor(tiles(b4), tiles(b4), ps[:, BR, SEQ:2 * SEQ].rearrange("p (t d) -> p t d", t=TILES), ALU.add).then_inc(S["x_ok"], 1)

                def prepare(e):
                    for k in range(1 + layer):
                        dve.wait_ge(up_hi, EXPERTS * layer + e * (1 + layer) + k + 1)
                        nc.vector.tensor_tensor(up_w(k, 1, e), up_raw(k, e), up_w(k, 0, e).bitcast(F32), ALU.subtract).then_inc(up_split, 1)

                def feed_forward(at, slot):
                    b0, b1, b2 = at(0), at(1), at(2)
                    b, e = (b1, slot - 3) if slot >= 3 else (b2, slot + EXPERTS - 3)
                    if b.exists:
                        after(dve, F["y_ps"], b, EXPERTS, e + 1, base)
                        after(dve, *((F["x_ok"], b, EXPERTS, e) if e else (F["g_ok"], b, 1, 1)), base)
                        for t in range(TILES):
                            ins = nc.vector.scalar_tensor_tensor(out=one_tile(b, t), in0=ps[:, BYS[layer][e % 2], t * P:(t + 1) * P], scalar=g_pad[:, b.ring, t, e:e + 1],
                                                                 in1=one_tile(b, t), op0=ALU.mult, op1=ALU.add)
                        ins.then_inc(F["x_ok"], 1)
                    if slot == 6 and b1.exists and layer == 0:
                        after(dve, F["y9_ps"], b1, 1, 1, base)
                        after(dve, F["x_ok"], b1, EXPERTS, e + 1, base)
                        nc.vector.tensor_tensor(tiles(b1), tiles(b1), ps[:, BG, SEQ:2 * SEQ].rearrange("p (t d) -> p t d", t=TILES), ALU.add).then_inc(F["y9_ok"], 1)
                        after(dve, F["y9_ok"], b1, 1, 1, base)
                    if b1.exists and layer == 1:
                        e = slot
                        after(dve, F["silu_ok"], b1, EXPERTS, e + 1, 0)
                        if e >= HIDS:
                            after(dve, F["y_ps"], b1, EXPERTS, e - HIDS + 1, base)
                        else:
                            after(dve, F["y_ps"], b2, EXPERTS, EXPERTS - HIDS + 1 + e, base)
                        nc.vector.tensor_tensor(hid[:, e % HIDS, :, :].rearrange("p c t -> p (c t)"), silu[:, e % 2, :, :].rearrange("p c t -> p (c t)"), ps[:, U1[e % 2], :], ALU.mult).then_inc(F["hid_ok"], 1)
                    if slot == 0 and b0.exists:
                        if b0.least == 0 and layer == 0:
                            dve.wait_ge(w_gate_in, 64)
                            link(nc.vector.tensor_copy(gate_hi[:, :, :], gate_raw[:, :, :]))
                            nc.vector.tensor_tensor(gate_lo[:, :, :], gate_raw[:, :, :], gate_hi[:, :, :].bitcast(F32), ALU.subtract).then_inc(w_split, 1)
                        stats_of(b0, F)
                    if slot == 1 and b0.exists:
                        after(dve, F["t_ps"], b1, 1, 1, base)
                        norm_of(b0)
                    if slot == 3 and b0.exists:
                        norm_t_lo(b0, F)
                    if slot >= 5 and b0.exists:
                        top_two(b0, slot - 5)

                def top_two(b, part):
                    count = [(0, 5, 11)[part]]

                    def chained(ins):
                        count[0] += 1
                        ins.then_inc(F["top"], 1)
                        after(dve, F["top"], b, TOP, count[0], base)

                    def wide(s):
                        return s[:, :].unsqueeze(2).broadcast_to([P, TILES, EXPERTS])

                    def first_of(hot, key, mk, se):
                        chained(nc.vector.tensor_tensor(gt[key][:, :, :], gt[hot][:, :, :], rank[:, :, :], ALU.mult))
                        chained(nc.vector.tensor_reduce(gs[mk][:, :], gt[key][:, :, :], AX.X, ALU.max))
                        chained(nc.vector.tensor_tensor(gt[se][:, :, :], gt[key][:, :, :], wide(gs[mk]), ALU.is_equal))

                    if part == 0:
                        logits = ps[:, BG, 0:TILES * EXPERTS].rearrange("p (t e) -> p t e", t=TILES)
                        after(dve, F["lg_ps"], b, 1, 1, base)
                        chained(nc.vector.tensor_reduce(gs["v1"][:, :], logits, AX.X, ALU.max))
                        nc.vector.tensor_tensor(gt["t"][:, :, :], logits, wide(gs["v1"]), ALU.subtract).then_inc(F["t_ok"], 1)
                        after(dve, F["t_ok"], b, 1, 1, base)
                        chained(nc.vector.tensor_scalar(gt["hot"][:, :, :], gt["t"][:, :, :], 0.0, None, ALU.is_ge))
                        first_of("hot", "key", "mk1", "sel1")
                    elif part == 1:
                        chained(nc.vector.scalar_tensor_tensor(out=gt["t2"][:, :, :], in0=gt["sel1"][:, :, :], scalar=-3e38, in1=gt["t"][:, :, :], op0=ALU.mult, op1=ALU.add))
                        chained(nc.vector.tensor_reduce(gs["v2"][:, :], gt["t2"][:, :, :], AX.X, ALU.max))
                        chained(nc.vector.tensor_tensor(gt["hot2"][:, :, :], gt["t2"][:, :, :], wide(gs["v2"]), ALU.is_ge))
                        first_of("hot2", "key2", "mk2", "sel2")
                    else:
                        chained(nc.vector.tensor_tensor(gt["both"][:, :, :], gt["sel1"][:, :, :], gt["sel2"][:, :, :], ALU.add))
                        after(dve, F["e_ok"], b, 1, 1, base)
                        chained(nc.vector.tensor_tensor(gt["we"][:, :, :], gt["both"][:, :, :], gt["e"][:, :, :], ALU.mult))
                        chained(nc.vector.tensor_reduce(gs["sum"][:, :], gt["we"][:, :, :], AX.X, ALU.add))
                        chained(nc.vector.reciprocal(gs["rsum"][:, :], gs["sum"][:, :]))
                        assert count[0] == TOP
                        nc.vector.tensor_tensor(g_pad[:, b.ring, :, 0:EXPERTS], gt["we"][:, :, :], wide(gs["rsum"]), ALU.mult).then_inc(F["g_ok"], 1)
                return attention, prepare, feed_forward

            run(dve, BATCHES, [parts(0), parts(1)])


def kernel(**inputs):
    import numpy as _np
    import concourse.bacc as _bacc
    from concourse.bass_utils import run_bass_kernel_spmd as _run

    nc = _bacc.Bacc("TRN2", target_bir_lowering=False, num_devices=1)
    arrays = {}

    def dram(name, a):
        a = _np.ascontiguousarray(a)
        arrays[name] = a
        return nc.dram_tensor(name, a.shape, mybir.dt.from_np(a.dtype), kind="ExternalInput").ap()

    i = {k: _np.asarray(v) for k, v in inputs.items()}
    w0, w1 = i["L0_attn_attn_W"], i["L1_attn_qkv_w"]
    b0, b1 = i["L0_attn_attn_b"], i["L1_attn_qkv_b"]

    def columns(a):
        return _np.concatenate([a[:, 0:2].transpose(0, 1, 2, 4, 3).reshape(len(a), 2, D), a[:, 2:3].transpose(0, 1, 3, 2, 4).reshape(len(a), 1, D)], 1)
    qkv_b = (columns(b0.reshape(1, SLOTS, GROUPS, 3, HD).transpose(0, 3, 1, 2, 4))[0], columns(b1.reshape(1, 3, SLOTS, GROUPS, HD))[0])
    w = {
        "qkv_w": [dram("qkv_w0", columns(w0.reshape(D, SLOTS, GROUPS, 3, HD).transpose(0, 3, 1, 2, 4))),
                  dram("qkv_w1", columns(w1.reshape(D, 3, SLOTS, GROUPS, HD)))],
        "qk_b": [dram(f"qk_b{k}", b[0:2].T) for k, b in enumerate(qkv_b)],
        "v_b": [dram("v_b0", b0.reshape(HEADS, 3, HD)[:, 2].reshape(D, 1)), dram("v_b1", b1[2 * D:].reshape(D, 1))],
        "out_w": [dram("out_w0", i["L0_attn_out_W"]), dram("out_w1", i["L1_attn_out_w"])],
        "out_b": [dram("out_b0", i["L0_attn_out_b"]), dram("out_b1", i["L1_attn_out_b"])],
        "gate": [dram("gate0", i["L0_ffn_gate"]), dram("gate1", i["L1_ffn_gate_kernel"])],
        "up": [[dram("up0", i["L0_ffn_W1"])], [dram("up1", i["L1_ffn_w0_kernel"]), dram("up2", i["L1_ffn_w1_kernel"])]],
        "down": [dram("down0", i["L0_ffn_W2"]), dram("down1", i["L1_ffn_wo_kernel"])],
        "b1": dram("b1", i["L0_ffn_b1"].reshape(EXPERTS, CHUNKS, P).transpose(2, 0, 1)),
        "b2": dram("b2", i["L0_ffn_b2"]),
    }
    x = dram("x", i["L0_attn_encodings"])
    out = nc.dram_tensor("out", x.shape, F32, kind="ExternalOutput").ap()
    build(nc, w, x, out)
    r = _run(nc, [arrays], core_ids=[0])
    return r.results[0]["out"]
```
